# Optimizing a Trainium2 kernel written in Bass

```python
import numpy as np
import jax
import jax.numpy as jnp

def _softmax(x, axis=-1):
    return jax.nn.softmax(x, axis=axis)
def _gelu(x):
    return jax.nn.gelu(x, approximate=True)
def _silu(x):
    return jax.nn.silu(x)
def _sigmoid(x):
    return jax.nn.sigmoid(x)
def _layernorm(x, axis=-1, eps=1e-5):
    m = jnp.mean(x, axis=axis, keepdims=True)
    v = jnp.var(x, axis=axis, keepdims=True)
    return (x - m) / jnp.sqrt(v + eps)
def _scatter_add(tgt, idx, src, axis=0):
    return tgt.at[idx].add(src)
def _segment_sum(src, seg, n):
    return jax.ops.segment_sum(src, seg, n)

kernel_name = 'mk_conv_preact_d1_conv_nchw128_13a5b9'

def setup_inputs(seed: int = 0):
    np.random.seed(seed)
    _w = jnp.asarray
    def _rec_inputs():
        import jax
        import jax.numpy as jnp
        _gk = jax.random.key(seed)
        x = -0.0003929 + 0.9999 * jax.random.normal(jax.random.fold_in(_gk, 1), (2, 128, 256, 256), jnp.float32)
        return x
    x = _rec_inputs()
    def _L0_conv_setup():
        import jax, jax.numpy as jnp
        import numpy as np
        H, N, LMAX, KCH = (128, 64, 256, 2)

        def _ssm_kernel(A_re, A_im, C_re, C_im, log_dt, L):
            A = A_re + 1j * A_im
            C = C_re + 1j * C_im
            dt = jnp.exp(log_dt)
            dtA = dt[:, None] * A
            K = C * (jnp.exp(dtA) - 1.0) / A
            vand = jnp.exp(dtA[:, :, None] * jnp.arange(L, dtype=dtA.real.dtype))
            return 2.0 * jnp.einsum('chn,hnl->chl', K, vand).real

        def _bidir_pad(k, L_in):
            k0, k1 = (k[:1], k[1:])
            fwd = jnp.pad(k0, ((0, 0), (0, 0), (0, L_in)))
            bwd = jnp.pad(k1[..., ::-1], ((0, 0), (0, 0), (L_in, 0)))
            return fwd + bwd
        key = jax.random.key(seed)
        ks = jax.random.split(key, 8)
        B, L1, L2 = (2, 256, 256)
        u = jax.random.normal(ks[0], (B, H, L1, L2), jnp.float32)
        D = jax.random.normal(ks[1], (1, H), jnp.float32)

        def kparams(k_c, k_ci, k_dt):
            A_re = -0.5 * jnp.ones((H, N), jnp.float32)
            A_im = jnp.pi * jnp.broadcast_to(jnp.arange(N, dtype=jnp.float32), (H, N))
            C_re = jax.random.normal(k_c, (KCH, H, N), jnp.float32) * 0.5 ** 0.5
            C_im = jax.random.normal(k_ci, (KCH, H, N), jnp.float32) * 0.5 ** 0.5
            log_dt = jax.random.uniform(k_dt, (H,), jnp.float32, minval=np.log(0.001), maxval=np.log(0.1))
            return (A_re, A_im, C_re, C_im, log_dt)
        A_re0, A_im0, C_re0, C_im0, log_dt0 = kparams(ks[2], ks[3], ks[4])
        A_re1, A_im1, C_re1, C_im1, log_dt1 = kparams(ks[5], ks[6], ks[7])
        return {'u': u, 'D': D, 'A_re0': A_re0, 'A_im0': A_im0, 'C_re0': C_re0, 'C_im0': C_im0, 'log_dt0': log_dt0, 'A_re1': A_re1, 'A_im1': A_im1, 'C_re1': C_re1, 'C_im1': C_im1, 'log_dt1': log_dt1}
    _L0_conv_all = _L0_conv_setup()
    _L0_conv_in = {k: v for k, v in _L0_conv_all.items() if k in ('D', 'A_re0', 'A_im0', 'C_re0', 'C_im0', 'log_dt0', 'A_re1', 'A_im1', 'C_re1', 'C_im1', 'log_dt1', )}
    del _L0_conv_all

    return {
        "x": x,
        "L0_conv_D": _L0_conv_in["D"],
        "L0_conv_A_re0": _L0_conv_in["A_re0"],
        "L0_conv_A_im0": _L0_conv_in["A_im0"],
        "L0_conv_C_re0": _L0_conv_in["C_re0"],
        "L0_conv_C_im0": _L0_conv_in["C_im0"],
        "L0_conv_log_dt0": _L0_conv_in["log_dt0"],
        "L0_conv_A_re1": _L0_conv_in["A_re1"],
        "L0_conv_A_im1": _L0_conv_in["A_im1"],
        "L0_conv_C_re1": _L0_conv_in["C_re1"],
        "L0_conv_C_im1": _L0_conv_in["C_im1"],
        "L0_conv_log_dt1": _L0_conv_in["log_dt1"],
    }

def reference(x, L0_conv_D, L0_conv_A_re0, L0_conv_A_im0, L0_conv_C_re0, L0_conv_C_im0, L0_conv_log_dt0, L0_conv_A_re1, L0_conv_A_im1, L0_conv_C_re1, L0_conv_C_im1, L0_conv_log_dt1):
    import jax
    import jax.numpy as jnp
    def _L0_conv_ref(u, D, A_re0, A_im0, C_re0, C_im0, log_dt0, A_re1, A_im1, C_re1, C_im1, log_dt1):
        import jax, jax.numpy as jnp
        import numpy as np
        H, N, LMAX, KCH = (128, 64, 256, 2)

        def _ssm_kernel(A_re, A_im, C_re, C_im, log_dt, L):
            A = A_re + 1j * A_im
            C = C_re + 1j * C_im
            dt = jnp.exp(log_dt)
            dtA = dt[:, None] * A
            K = C * (jnp.exp(dtA) - 1.0) / A
            vand = jnp.exp(dtA[:, :, None] * jnp.arange(L, dtype=dtA.real.dtype))
            return 2.0 * jnp.einsum('chn,hnl->chl', K, vand).real

        def _bidir_pad(k, L_in):
            k0, k1 = (k[:1], k[1:])
            fwd = jnp.pad(k0, ((0, 0), (0, 0), (0, L_in)))
            bwd = jnp.pad(k1[..., ::-1], ((0, 0), (0, 0), (L_in, 0)))
            return fwd + bwd
        B, _, L1, L2 = u.shape
        Lk1, Lk2 = (min(L1, LMAX), min(L2, LMAX))
        k1 = _bidir_pad(_ssm_kernel(A_re0, A_im0, C_re0, C_im0, log_dt0, Lk1), L1)
        k2 = _bidir_pad(_ssm_kernel(A_re1, A_im1, C_re1, C_im1, log_dt1, Lk2), L2)
        P1, P2 = (L1 + Lk1, L2 + Lk2)
        u_f = jnp.fft.rfftn(u, s=(P1, P2), axes=(-2, -1))
        kf1 = jnp.fft.fft(k1, n=P1, axis=-1)
        kf2 = jnp.fft.rfft(k2, n=P2, axis=-1)
        k_f = jnp.einsum('chm,chn->chmn', kf1, kf2)
        y_f = jnp.einsum('bhmn,chmn->bchmn', u_f, k_f)
        y = jnp.fft.irfftn(y_f, s=(P1, P2), axes=(-2, -1))[..., :L1, :L2]
        y = y + jnp.einsum('bhxy,ch->bchxy', u, D)
        return y.reshape(B, -1, L1, L2)

    def _gn(v, G=32, eps=1e-5):
        B_, C_, H_, W_ = v.shape
        g = v.reshape(B_, G, C_ // G, H_, W_)
        m = jnp.mean(g, axis=(2, 3, 4), keepdims=True)
        s = jnp.var(g, axis=(2, 3, 4), keepdims=True)
        return ((g - m) / jnp.sqrt(s + eps)).reshape(v.shape)

    def _ln_c(v, eps=1e-6):
        m = jnp.mean(v, axis=1, keepdims=True)
        s = jnp.var(v, axis=1, keepdims=True)
        return (v - m) / jnp.sqrt(s + eps)

    def _ln_t(v, eps=1e-5):
        m = jnp.mean(v, axis=-1, keepdims=True)
        s = jnp.var(v, axis=-1, keepdims=True)
        return (v - m) / jnp.sqrt(s + eps)

    def _to_tokens(v):
        B_, C_, H_, W_ = v.shape
        return v.reshape(B_, C_, H_ * W_).transpose(0, 2, 1)
    def _from_tokens(t, like):
        B_, C_, H_, W_ = like.shape
        return t.transpose(0, 2, 1).reshape(B_, C_, H_, W_)

    x = x + _L0_conv_ref(_gn(x), L0_conv_D, L0_conv_A_re0, L0_conv_A_im0, L0_conv_C_re0, L0_conv_C_im0, L0_conv_log_dt0, L0_conv_A_re1, L0_conv_A_im1, L0_conv_C_re1, L0_conv_C_im1, L0_conv_log_dt1)
    return x


_drawn_inputs = setup_inputs


def setup_inputs(seed=0):
    import zlib

    import numpy as np

    out = dict(_drawn_inputs(seed))
    spreads = {'L0_conv_A_re0': (-0.5, 0.2), 'L0_conv_A_re1': (-0.5, 0.2)}
    factors = {}
    for name, (base, spread) in spreads.items():
        noise = np.random.default_rng([zlib.crc32(name.encode()), seed]).standard_normal(out[name].shape)
        drawn = base * np.exp(spread * noise) if base else spread * noise
        out[name] = jnp.asarray(drawn.astype(out[name].dtype))
    for name, factor in factors.items():
        out[name] = (out[name] * factor).astype(out[name].dtype)
    return out
```

```python
import math
from contextlib import ExitStack

import concourse.bass as bass
from concourse import mybir

ALU = mybir.AluOpType
ACT = mybir.ActivationFunctionType
AX = mybir.AxisListType
F32 = mybir.dt.float32
F16 = mybir.dt.float16
I32 = mybir.dt.int32

P = 128
B, C, L = 2, 128, 256
N = 64
GC = 4
G = C // GC
UNITS = G * B
PAIRS = UNITS * 2
LOW, HIGH = 32, 8
U_SCALE = 64.0
T_SCALE = float(2 ** 15)
Z_SCALE = 2.0 ** -15
Y_SCALE = 1.0 / (U_SCALE * T_SCALE * Z_SCALE * T_SCALE)
GN_EPS = 1e-5
TINY = 1e-30
MAGIC = 1.5 * 2 ** 23
TWO_PI = 2.0 * math.pi
TP1 = 6.28125
TP2 = float(round((TWO_PI - TP1) * 2 ** 22) / 2 ** 22)
TP3 = TWO_PI - TP1 - TP2
LN2_HI = 0.693359375
LN2_LO = math.log(2.0) - LN2_HI
SPLIT_LEAD = 3
CHAIN_LEAD = 5
STAT_LEAD = 7
BODY = 8
W_COLS = L + 2


def conv_block(nc, x, D, A_re, A_im, C_re, C_im, log_dt, out):
    x_v = x.rearrange("b (g c) (p s) w -> b g p c (s w)", c=GC, s=2)
    out_v = out.rearrange("b (g c) (p s) w -> b g p c (s w)", c=GC, s=2)
    v_dram = nc.dram_tensor("v_rows", [C, 4, 2 * L], F16, kind="Internal")
    y_dram = nc.dram_tensor("y_factor", [2, C // 2], F32, kind="Internal")

    ctx = ExitStack()
    with ctx:
        def sb(name, shape, dt=F32, where=ctx):
            return where.enter_context(nc.sbuf_tensor(name, shape, dt))

        def pb(name, shape, where=ctx):
            return where.enter_context(nc.psum_tensor(name, shape, F32))

        def sem(name):
            return ctx.enter_context(nc.semaphore(name))

        x_sb = sb("x_sb", [P, 4, GC, 2 * L])
        W = sb("W", [P, 2, GC * 4, W_COLS], F16)
        d_bc = sb("d_bc", [P, C])
        y_bc = sb("y_bc", [P, C])
        ones_neg = sb("ones_neg", [P, P])
        ones_pos = sb("ones_pos", [P, P])
        eps_gn = sb("eps_gn", [P, 1])

        gen = ExitStack()
        a_in = sb("a_in", [P, 2, 2, N], where=gen)
        c_in = sb("c_in", [P, 2, 2, 2, N], where=gen)
        ldt = sb("ldt", [P, 2], where=gen)
        dt = sb("dt", [P, 2], where=gen)
        dt_pow = sb("dt_pow", [P, 2], where=gen)
        xz = sb("xz", [P, 2 * N], where=gen)
        th = sb("th", [P, 2 * N], where=gen)
        tau = sb("tau", [P, 2 * N], where=gen)
        em = sb("em", [P, 2 * N], where=gen)
        sin1 = sb("sin1", [P, 2 * N], where=gen)
        sinh = sb("sinh", [P, 2 * N], where=gen)
        wk = sb("wk", [P, 8, 2 * N], where=gen)
        srcs = sb("srcs", [P, 14, 2, N], where=gen)
        turned = sb("turned", [P, 14, P], where=gen)
        ident = sb("ident", [P, P], where=gen)
        swap = sb("swap", [P, P], where=gen)
        phase = sb("phase", [P, 1], where=gen)
        tab = sb("tab", [P, LOW + HIGH, 2 * P], where=gen)
        mod = sb("mod", [P, LOW + HIGH, 2 * P], where=gen)
        whole = sb("whole", [P, 2, HIGH, 2 * P], where=gen)
        g_a = mod[:, 8:24, :].rearrange("p (c a) h -> p c a h", c=2)
        g_b = mod[:, 24:40, :].rearrange("p (c a) h -> p c a h", c=2)
        gb = sb("gb", [P, C // 2, 2, HIGH], where=gen)
        g32 = sb("g32", [C // 2, 4, 2 * L], where=gen)
        gabs = sb("gabs", [C // 2, 2 * L], where=gen)
        l1 = sb("l1", [C // 2, 4], where=gen)
        rl1 = sb("rl1", [C // 2, 4], where=gen)
        yf = sb("yf", [C // 2, 2], where=gen)
        v16 = sb("v16", [C // 2, 4, 2, 2 * L], F16, where=gen)
        gen.close()

        u_sb = sb("u_sb", [P, 4, 4, 2, P])
        xh = sb("xh", [P, 4, 4, 2, P], F16)
        xl = sb("xl", [P, 4, 4, 2, P], F16)
        zh = sb("zh", [P, 2, 4, 2, P], F16)
        zl = sb("zl", [P, 2, 4, 2, P], F16)
        t_sb = sb("t_sb", [P, 4, GC, 2 * L])
        bst = sb("bst", [P, 2, GC, 6])
        mv = sb("mv", [P, 2, 2])
        negm = sb("negm", [P, 2])
        dev = sb("dev", [P, 2])
        ve = sb("ve", [P, 2])
        sd = sb("sd", [P, 2])
        r0 = sb("r0", [P, 2])
        nw = sb("nw", [P, 2, 4])
        d_unit = sb("d_unit", [P, 2, GC])
        coef = sb("coef", [P, 4, 2 + 3 * GC])

        genp = ExitStack()
        p_turn = pb("p_turn", [P, 4, 512], where=genp)
        p_mode = pb("p_mode", [P, C // 2, 2 * HIGH], where=genp)
        genp.close()
        genq = ExitStack()
        p_rows = pb("p_rows", [C // 2, 2, HIGH, P], where=genq)
        genq.close()
        z_ps = pb("z_ps", [P, 2, 2, 512])
        y_ps = pb("y_ps", [P, 2, 512])
        st_ps = pb("st_ps", [P, 512])

        s_in = sem("params_loaded")
        s_dbc = sem("d_broadcast")
        s_const = sem("constants_ready")
        s_v = sem("vector_chain")
        s_tau = sem("tau_ready")
        s_sin = sem("mode_sines_ready")
        s_srcs = sem("srcs_ready")
        s_turn = sem("turned_in_psum")
        s_turned = sem("turned_in_sbuf")
        s_mod = sem("moduli_ready")
        s_whole = sem("whole_turns_ready")
        s_frac = sem("fractions_ready")
        s_sine = sem("sines_ready")
        s_tab = sem("tables_ready")
        s_swap = sem("exchanged_in_psum")
        s_ga = sem("g_a_ready")
        s_g = sem("g_ready")
        s_mode = sem("mode_sums_in_psum")
        s_gb = sem("mode_sums_in_sbuf")
        s_rows = sem("rows_in_psum")
        s_g32 = sem("rows_in_sbuf")
        s_l1 = sem("absolute_sums_ready")
        s_v16 = sem("v_rows_ready")
        s_vout = sem("v_rows_stored")
        s_ybc = sem("y_factor_broadcast")

        x_loaded = [sem(f"x_loaded{i}") for i in range(4)]
        w_loaded = [sem(f"w_loaded{i}") for i in range(2)]
        stored = [sem(f"stored{i}") for i in range(4)]
        bn_done = sem("bn_done")
        agg_done = sem("agg_done")
        mean_ps = sem("mean_ps")
        negm_done = sem("negm_done")
        dev_done = sem("dev_done")
        var_ps = sem("var_ps")
        ve_done = sem("ve_done")
        sd_done = sem("sd_done")
        rec_done = sem("rec_done")
        nw_done = sem("newton_chain")
        du_done = sem("d_unit_done")
        coef_done = sem("coef_done")
        u_done = sem("u_done")
        xh_done = sem("xh_done")
        xl_done = sem("xl_done")
        t_done = sem("t_done")
        s1_done = sem("first_product_done")
        zh_done = sem("zh_done")
        zl_done = sem("zl_done")
        s2_done = sem("second_product_done")
        y_free = sem("y_banks_free")

        block = ctx.enter_context(nc.Block())

        TURNS = PAIRS // BODY

        def exists(it, j):
            return not isinstance(it, int) or 0 <= BODY * it + j < PAIRS

        def least(value):
            return max(value, 0) if isinstance(value, int) else value

        def run_steps(eng, step):
            for j in range(-STAT_LEAD, BODY):
                step(0, j)
            with eng.Fori(1, TURNS - 1) as it:
                for j in range(BODY):
                    step(it, j)
            for j in range(BODY):
                step(TURNS - 1, j)

        @block.sync
        def _(sp):
            with nc.allow_non_contiguous_dma(reason="two numbers per channel"):
                for a in range(2):
                    sp.dma_start(ldt[:, a:a + 1], log_dt[a].rearrange("(h o) -> h o", o=1)).then_inc(s_in, 16)
            for a in range(2):
                sp.dma_start(a_in[:, 0, a, :], A_re[a]).then_inc(s_in, 16)
                sp.dma_start(a_in[:, 1, a, :], A_im[a]).then_inc(s_in, 16)
            for a in range(2):
                sp.dma_start(c_in[:, :, 0, a, :], C_re[a].rearrange("c h n -> h c n")).then_inc(s_in, 16)
                sp.dma_start(c_in[:, :, 1, a, :], C_im[a].rearrange("c h n -> h c n")).then_inc(s_in, 16)
            sp.dma_start(d_bc[:, :], D.partition_broadcast(P)).then_inc(s_dbc, 16)

            def load_x(v, g):
                sp.dma_start(x_sb[:, v, :, :], x_v[v % 2, g]).then_inc(x_loaded[v], 16)

            def load_w(slot, g):
                rows = bass.AP(v_dram, g * (GC * 4 * 2 * L), [[2, P], [2 * L, GC * 4], [1, W_COLS]])
                sp.dma_start(W[:, slot, :, :], rows).then_inc(w_loaded[slot], 16)

            for v in range(4):
                load_x(v, v // 2)
            sp.wait_ge(s_v16, 9)
            sp.dma_start(v_dram.ap().rearrange("(e h) r m -> h e (r m)", e=2),
                         v16[:, :, :, :].rearrange("h (e a) l m -> h e (a l m)", e=2)).then_inc(s_vout, 16)
            with nc.allow_non_contiguous_dma(reason="one number per channel"):
                sp.dma_start(y_dram.ap().rearrange("e h -> h e"), yf[:, :]).then_inc(s_vout, 16)
            sp.wait_ge(s_vout, 32)
            load_w(0, 0)
            sp.dma_start(y_bc[:, :], y_dram.ap().rearrange("e h -> (e h)").partition_broadcast(P)
                         ).then_inc(s_ybc, 16)
            load_w(1, 1)

            def store(it, v):
                sp.wait_ge(y_free, it * (2 * BODY) + 4 * v + 6)
                sp.dma_start(out_v[v % 2, it * 2 + v // 2], t_sb[:, v % 4, :, :]).then_inc(stored[v % 4], 16)

            def unit(it, v, first, last):
                if not last:
                    sp.wait_ge(u_done, it * BODY + 2 * v + 2)
                    sp.wait_ge(t_done, it * BODY + 2 * v + 2)
                    load_x(v, it * 2 + 2 + v // 2)
                if v or not first:
                    store(it, v - 1)
                if v % 2 == 0 and not (first and v == 0) and not (last and v == 2):
                    sp.wait_ge(s2_done, it * (2 * BODY) + 4 * v)
                    load_w((v // 2 + 1) % 2, it * 2 + v // 2 + 1)

            for v in range(4):
                unit(0, v, True, False)
            with sp.Fori(1, TURNS - 1) as it:
                for v in range(4):
                    unit(it, v, False, False)
            for v in range(4):
                unit(TURNS - 1, v, False, True)
            store(TURNS - 1, 3)
            for v in range(4):
                sp.wait_ge(stored[v], 16 * TURNS)

        @block.gpsimd
        def _(pool):
            pool.memset(ident[:, :], 0.0).then_inc(s_const, 1)
            pool.memset(ones_neg[:, :], -1.0 / P).then_inc(s_const, 1)
            pool.memset(ones_pos[:, :], 1.0 / P).then_inc(s_const, 1)
            pool.memset(eps_gn[:, :], GN_EPS).then_inc(s_const, 1)
            pool.wait_ge(s_const, 4)
            pool.affine_select(out=ident[:, :], in_=ident[:, :], compare_op=ALU.not_equal, fill=1.0,
                               base=0, pattern=[[-1, P]], channel_multiplier=1).then_inc(s_const, 1)
            pool.wait_ge(s_const, 5)
            pool.tensor_copy(swap[:, 0:N], ident[:, N:P]).then_inc(s_const, 1)
            pool.tensor_copy(swap[:, N:P], ident[:, 0:N]).then_inc(s_const, 1)

            pool.wait_ge(s_turned, 4)
            pool.wait_ge(s_tab, 5)
            for c in range(2):
                k_a = turned[:, 6 + 2 * c:8 + 2 * c, :].rearrange("p a h -> p (a h)")
                pool.tensor_tensor(g_a[:, c, :, :], tab[:, 0:HIGH, :],
                                   k_a.unsqueeze(1).to_broadcast([P, HIGH, 2 * P]), ALU.mult).then_inc(s_ga, 1)
            pool.wait_ge(s_ybc, 16)
            pool.wait_ge(s_dbc, 16)

            def newton(it, v, dit):
                k = v % 2
                n = it * 4 + (4 * dit + v)
                g = it * 2 + (2 * dit + v // 2)
                t = [nw[:, k, i:i + 1] for i in range(4)]
                m, r = negm[:, k:k + 1], t[3]
                pool.tensor_copy(coef[:, v, 2 + 2 * GC:2 + 3 * GC],
                                 y_bc[:, bass.ds(g * GC, GC)]).then_inc(coef_done, 1)
                pool.tensor_copy(d_unit[:, k, :], d_bc[:, bass.ds(g * GC, GC)]).then_inc(du_done, 1)
                pool.wait_ge(rec_done, n + 1)
                pool.tensor_tensor(t[0], r0[:, k:k + 1], r0[:, k:k + 1], ALU.mult).then_inc(nw_done, 1)
                pool.wait_ge(nw_done, n * 4 + 1)
                pool.tensor_tensor(t[1], t[0], ve[:, k:k + 1], ALU.mult).then_inc(nw_done, 1)
                pool.wait_ge(nw_done, n * 4 + 2)
                pool.nop(nofuse=True)
                pool.tensor_scalar(t[2], t[1], -0.5, 1.5, ALU.mult, ALU.add).then_inc(nw_done, 1)
                pool.wait_ge(nw_done, n * 4 + 3)
                pool.tensor_tensor(r, t[2], r0[:, k:k + 1], ALU.mult).then_inc(nw_done, 1)
                pool.wait_ge(nw_done, n * 4 + 4)
                pool.wait_ge(du_done, n + 1)
                pool.nop(nofuse=True)
                pool.tensor_scalar(coef[:, v, 0:1], r, U_SCALE, None, ALU.mult).then_inc(coef_done, 1)
                pool.tensor_scalar(coef[:, v, 1:2], r, m, U_SCALE, ALU.mult, ALU.mult).then_inc(coef_done, 1)
                pool.tensor_scalar(coef[:, v, 2:2 + GC], d_unit[:, k, :], r, 1.0,
                                   ALU.mult, ALU.add).then_inc(coef_done, 1)
                pool.tensor_scalar(coef[:, v, 2 + GC:2 + 2 * GC], d_unit[:, k, :], r, m,
                                   ALU.mult, ALU.mult).then_inc(coef_done, 1)

            def step(it, j):
                if exists(it, j + SPLIT_LEAD):
                    jj = j + SPLIT_LEAD
                    n = it * BODY + jj
                    v = jj // 2 % 4
                    pool.wait_ge(xh_done, n + 1)
                    pool.wait_ge(s1_done, least(n - 3))
                    pool.tensor_tensor(xl[:, jj % 4], u_sb[:, jj % 4], xh[:, jj % 4], ALU.subtract
                                       ).then_inc(xl_done, 1)
                    pool.wait_ge(stored[v], least(it * 16 + 16 * (jj // BODY)))
                    pool.nop(nofuse=True)
                    for c in (2 * (jj % 2), 2 * (jj % 2) + 1):
                        ins = pool.tensor_scalar(t_sb[:, v, c, :], x_sb[:, v, c, :], coef[:, v, 2 + c:3 + c],
                                                 coef[:, v, 2 + GC + c:3 + GC + c], ALU.mult, ALU.add)
                    ins.then_inc(t_done, 1)
                if j % 2 and exists(it, j + CHAIN_LEAD):
                    newton(it, (j + CHAIN_LEAD) // 2 % 4, (j + CHAIN_LEAD) // BODY)

            run_steps(pool, step)

        @block.scalar
        def _(act):
            act.wait_ge(s_tau, 1)
            act.activation(sin1[:, :], tau[:, :], ACT.Sin, scale=TWO_PI)
            act.activation(sinh[:, :], tau[:, :], ACT.Sin, scale=math.pi).then_inc(s_sin, 1)
            for i, rows in enumerate(((0, 4), (4, 6), (6, 8), (8, 12), (12, 14))):
                if i in (0, 2):
                    act.wait_ge(s_turn, 1 + i // 2)
                r, e = rows
                act.activation(turned[:, r:e, :], p_turn[:, r // 4, 128 * (r % 4):128 * (r % 4) + 128 * (e - r)]
                               .rearrange("p (r h) -> p r h", h=P), ACT.Copy).then_inc(s_turned, 1)
                if i == 1:
                    act.wait_ge(s_turned, 2)
                    x_t = turned[:, 4:6, :].rearrange("p a h -> p (a h)")
                    for b in range(HIGH + LOW):
                        times = float(LOW * b if b < HIGH else b - HIGH)
                        act.activation(mod[:, b, :], x_t, ACT.Exp, scale=times).then_inc(s_mod, 1)
            for c in range(5):
                act.wait_ge(s_frac, c + 1)
                part = tab[:, 8 * c:8 * c + 8, :]
                act.activation(part, part, ACT.Sin, scale=TWO_PI).then_inc(s_sine, 1)
            act.wait_ge(s_mode, 1)
            act.activation(gb[:, :, :, :], p_mode[:, :, :], ACT.Copy).then_inc(s_gb, 1)
            act.wait_ge(s_g32, 4)
            for r in range(4):
                if r:
                    act.wait_ge(s_l1, r)
                act.activation(gabs[:, :], g32[:, r, :], ACT.Abs, accum_out=l1[:, r:r + 1]).then_inc(s_l1, 1)

            def step(it, j):
                chain = j % 2 and exists(it, j + CHAIN_LEAD)
                if chain:
                    k = (j + CHAIN_LEAD) // 2 % 2
                    n = it * 4 + (j + CHAIN_LEAD) // 2
                    act.wait_ge(mean_ps, n + 1)
                    act.activation(negm[:, k:k + 1], st_ps[:, 2 * k:2 * k + 1], ACT.Copy).then_inc(negm_done, 1)
                    act.wait_ge(negm_done, n + 1)
                    act.activation(dev[:, k:k + 1], mv[:, k, 0:1], ACT.Square, bias=negm[:, k:k + 1]
                                   ).then_inc(dev_done, 1)
                if exists(it, j + SPLIT_LEAD):
                    jj = j + SPLIT_LEAD
                    m = it * BODY + jj
                    v = jj // 2 % 4
                    act.wait_ge(coef_done, it * (5 * 4) + (5 * (jj // 2) + 5))
                    act.wait_ge(xl_done, least(m - 3))
                    c = 2 * (jj % 2)
                    act.activation(u_sb[:, jj % 4],
                                   x_sb[:, v, c:c + 2, :].rearrange("p c (s q t) -> p (c s) t q", s=2, t=2),
                                   ACT.Identity, bias=coef[:, v, 1:2], scale=coef[:, v, 0:1]).then_inc(u_done, 1)
                    act.wait_ge(u_done, m + 1)
                    act.wait_ge(s1_done, least(m - 3))
                    act.activation(xh[:, jj % 4], u_sb[:, jj % 4], ACT.Copy).then_inc(xh_done, 1)
                if exists(it, j + 1):
                    m = it * BODY + j
                    z = (j + 1) % 2
                    act.wait_ge(s1_done, m + 2)
                    act.wait_ge(s2_done, least(m * 2))
                    act.activation(zh[:, z], z_ps[:, z].rearrange("p i (a r t) -> p (i a) t r", a=2, t=2)
                                   [:, :, ::-1, ::-1], ACT.Copy, scale=Z_SCALE).then_inc(zh_done, 1)
                if chain:
                    act.wait_ge(var_ps, n + 1)
                    act.activation(ve[:, k:k + 1], st_ps[:, 2 * k + 1:2 * k + 2], ACT.Identity,
                                   bias=eps_gn[:, 0:1]).then_inc(ve_done, 1)
                    act.wait_ge(ve_done, n + 1)
                    act.activation(sd[:, k:k + 1], ve[:, k:k + 1], ACT.Sqrt).then_inc(sd_done, 1)

            run_steps(act, step)

        @block.tensor
        def _(pe):
            pe.wait_ge(s_const, 7)
            for i, rows in enumerate((range(6), range(6, 14))):
                pe.wait_ge(s_srcs, i + 1)
                if i == 1:
                    pe.wait_ge(s_turned, 2)
                for r in rows:
                    ins = pe.transpose(p_turn[:, r // 4, 128 * (r % 4):128 * (r % 4) + 128],
                                       srcs[:, r].rearrange("p a n -> p (a n)"), ident[:, :])
                ins.then_inc(s_turn, 1)
            pe.wait_ge(s_tab, 1)
            pe.wait_ge(s_turned, 5)
            for i in range(4):
                ins = pe.matmul(p_turn[:, i, :], swap[:, :],
                                tab[:, 2 * i:2 * i + 2, :].rearrange("p a h -> p (a h)"), start=True, stop=True)
            ins.then_inc(s_swap, 1)
            pe.wait_ge(s_g, 2)
            pe.wait_ge(s_tab, 5)
            for a in range(2):
                for h in range(C):
                    q, hs = 32 * (2 * a + h // (C // 2)), h % (C // 2)
                    ins = pe.matmul(p_mode[q:q + 32, hs, :], tab[:, HIGH:, a * P + h],
                                    g_b[:, :, :, a * P + h], start=True, stop=True)
            ins.then_inc(s_mode, 1)
            pe.wait_ge(s_gb, 1)
            for c in range(2):
                for a in range(HIGH):
                    ins = pe.transpose(p_rows[:, c, a, :], gb[:, :, c, a], ident[:, :])
            ins.then_inc(s_rows, 1)
            pe.wait_ge(s_g32, 4)

            def step(it, j):
                chain = j % 2 and exists(it, j + CHAIN_LEAD)
                if chain:
                    k = (j + CHAIN_LEAD) // 2 % 2
                    n = it * 4 + (j + CHAIN_LEAD) // 2
                    pe.wait_ge(agg_done, n + 1)
                    pe.matmul(st_ps[:, 2 * k:2 * k + 1], ones_neg[:, :], mv[:, k, 0:1],
                              start=True, stop=True).then_inc(mean_ps, 1)
                if exists(it, j + 1):
                    jj = j + 1
                    w = jj // 4 % 2
                    if jj % 4 == 0:
                        pe.wait_ge(w_loaded[w], it * 16 + 16 * (jj // BODY) + 16)
                    pe.wait_ge(xl_done, it * BODY + j + 2)
                    for i in range(2):
                        row = 4 * (2 * (jj % 2) + i)
                        for t in range(2):
                            n_mm = 0
                            for s in range(2):
                                for u, half in ((xh, 0), (xh, 1), (xl, 0)):
                                    ins = pe.matmul(z_ps[:, jj % 2, i, L * t:L * t + L], u[:, jj % 4, 2 * i + s, t, :],
                                                    W[:, w, row + half, s:s + L], start=n_mm == 0, stop=n_mm == 5)
                                    n_mm += 1
                    ins.then_inc(s1_done, 1)
                if chain:
                    pe.wait_ge(dev_done, n + 1)
                    pe.matmul(st_ps[:, 2 * k + 1:2 * k + 2], ones_pos[:, :], dev[:, k:k + 1], start=True, stop=False)
                    pe.matmul(st_ps[:, 2 * k + 1:2 * k + 2], ones_pos[:, :], mv[:, k, 1:2],
                              start=False, stop=True).then_inc(var_ps, 1)
                if exists(it, j):
                    w = j // 4 % 2
                    pe.wait_ge(zl_done, it * BODY + j + 1)
                    for i in range(2):
                        row = 4 * (2 * (j % 2) + i) + 2
                        pe.wait_ge(y_free, it * (2 * BODY) + 2 * j + i + 1)
                        for s in range(2):
                            n_mm = 0
                            for t in range(2):
                                for z, half in ((zh, 0), (zh, 1), (zl, 0)):
                                    ins = pe.matmul(y_ps[:, i, L * s:L * s + L], z[:, j % 2, 2 * i + t, s, :],
                                                    W[:, w, row + half, t:t + L], start=n_mm == 0, stop=n_mm == 5)
                                    n_mm += 1
                        ins.then_inc(s2_done, 1)

            run_steps(pe, step)

        @block.vector
        def _(dve):
            count = [0]

            def chain(ins):
                count[0] += 1
                ins.then_inc(s_v, 1)
                dve.wait_ge(s_v, count[0])

            def exp_parts(src, res, power, w):
                k, r = w
                chain(dve.tensor_scalar(r, src, -87.0, 88.0, ALU.max, ALU.min))
                chain(dve.tensor_scalar(k, r, 1.0 / math.log(2.0), MAGIC, ALU.mult, ALU.add))
                chain(dve.tensor_scalar(k, k, MAGIC, None, ALU.subtract))
                chain(dve.scalar_tensor_tensor(r, k, -LN2_HI, r, ALU.mult, ALU.add))
                chain(dve.scalar_tensor_tensor(r, k, -LN2_LO, r, ALU.mult, ALU.add))
                chain(dve.tensor_scalar(power.bitcast(I32), k, 127.0, float(2 ** 23), ALU.add, ALU.mult))
                chain(dve.tensor_scalar(res, r, 1.0 / 5040.0, None, ALU.mult))
                for f in (720.0, 120.0, 24.0, 6.0, 2.0, 1.0):
                    chain(dve.scalar_tensor_tensor(res, res, 1.0 / f, r, ALU.add, ALU.mult))

            w0, w1, w2, w3, w4, w5, w6, w7 = (wk[:, i, :] for i in range(8))
            chain(dve.memset(phase[0:N, :], 0.25))
            chain(dve.memset(phase[N:P, :], 0.0))
            dve.wait_ge(s_in, 32 + 64 + 64)
            exp_parts(ldt[:, :], dt[:, :], dt_pow[:, :], (wk[:, 0, 0:2], wk[:, 1, 0:2]))
            chain(dve.scalar_tensor_tensor(dt[:, :], dt[:, :], 1.0, dt_pow[:, :], ALU.add, ALU.mult))
            for a in range(2):
                dve.tensor_scalar(xz[:, a * N:a * N + N], a_in[:, 0, a, :], dt[:, a:a + 1], None, ALU.mult)
                chain(dve.tensor_scalar(th[:, a * N:a * N + N], a_in[:, 1, a, :], dt[:, a:a + 1], None, ALU.mult))
            chain(dve.tensor_scalar(w0, th[:, :], 1.0 / TWO_PI, MAGIC, ALU.mult, ALU.add))
            chain(dve.tensor_scalar(w0, w0, MAGIC, None, ALU.subtract))
            chain(dve.scalar_tensor_tensor(w1, w0, -TP1, th[:, :], ALU.mult, ALU.add))
            chain(dve.scalar_tensor_tensor(w1, w0, -TP2, w1, ALU.mult, ALU.add))
            chain(dve.scalar_tensor_tensor(w1, w0, -TP3, w1, ALU.mult, ALU.add))
            chain(dve.tensor_scalar(w1, w1, 1.0 / TWO_PI, -0.5, ALU.mult, ALU.max))
            chain(dve.tensor_scalar(tau[:, :], w1, 0.5, None, ALU.min))
            dve.engine_nop().then_inc(s_tau, 1)

            chain(dve.tensor_scalar(w0, tau[:, :], float(LOW), MAGIC, ALU.mult, ALU.add))
            chain(dve.tensor_scalar(w0, w0, MAGIC, None, ALU.subtract))
            for h in range(2):
                dve.tensor_copy(srcs[:, 0:2, h, :], tau[:, :].rearrange("p (a n) -> p a n", a=2))
                dve.tensor_copy(srcs[:, 4:6, h, :], xz[:, :].rearrange("p (a n) -> p a n", a=2))
                ins = dve.scalar_tensor_tensor(srcs[:, 2:4, h, :], tau[:, :].rearrange("p (a n) -> p a n", a=2),
                                               float(LOW), w0.rearrange("p (a n) -> p a n", a=2),
                                               ALU.mult, ALU.subtract)
            ins.then_inc(s_srcs, 1)

            exp_parts(xz[:, :], em[:, :], w2, (w0, w1))
            chain(dve.tensor_tensor(em[:, :], em[:, :], w2, ALU.mult))
            chain(dve.scalar_tensor_tensor(em[:, :], w2, -1.0, em[:, :], ALU.add, ALU.add))
            dve.wait_ge(s_sin, 1)
            chain(dve.scalar_tensor_tensor(w0, sinh[:, :], -2.0, sinh[:, :], ALU.mult, ALU.mult))
            chain(dve.scalar_tensor_tensor(w3, em[:, :], 1.0, w0, ALU.add, ALU.mult))
            chain(dve.tensor_tensor(w3, w3, em[:, :], ALU.add))
            chain(dve.scalar_tensor_tensor(w4, em[:, :], 1.0, sin1[:, :], ALU.add, ALU.mult))
            a_re = a_in[:, 0].rearrange("p a n -> p (a n)")
            a_im = a_in[:, 1].rearrange("p a n -> p (a n)")
            chain(dve.tensor_tensor(w0, a_re, a_re, ALU.mult))
            chain(dve.tensor_tensor(w1, a_im, a_im, ALU.mult))
            chain(dve.tensor_tensor(w0, w0, w1, ALU.add))
            chain(dve.reciprocal(w0, w0))
            chain(dve.tensor_tensor(w1, w3, a_re, ALU.mult))
            chain(dve.tensor_tensor(w2, w4, a_im, ALU.mult))
            chain(dve.tensor_tensor(w1, w1, w2, ALU.add))
            chain(dve.scalar_tensor_tensor(w5, w1, 2.0, w0, ALU.mult, ALU.mult))
            chain(dve.tensor_tensor(w1, w4, a_re, ALU.mult))
            chain(dve.tensor_tensor(w2, w3, a_im, ALU.mult))
            chain(dve.tensor_tensor(w1, w1, w2, ALU.subtract))
            chain(dve.scalar_tensor_tensor(w6, w1, 2.0, w0, ALU.mult, ALU.mult))
            for c in range(2):
                c_re = c_in[:, c, 0].rearrange("p a n -> p (a n)")
                c_im = c_in[:, c, 1].rearrange("p a n -> p (a n)")
                chain(dve.tensor_tensor(w0, c_re, w5, ALU.mult))
                chain(dve.tensor_tensor(w1, c_im, w6, ALU.mult))
                chain(dve.tensor_tensor(w2, w0, w1, ALU.subtract))
                chain(dve.tensor_tensor(w0, c_re, w6, ALU.mult))
                chain(dve.tensor_tensor(w1, c_im, w5, ALU.mult))
                chain(dve.tensor_tensor(w3, w0, w1, ALU.add))
                k_re = w2.rearrange("p (a n) -> p a n", a=2)
                k_im = w3.rearrange("p (a n) -> p a n", a=2)
                a_row, b_row = 6 + 2 * c, 10 + 2 * c
                dve.tensor_copy(srcs[:, a_row:a_row + 2, 0, :], k_re)
                dve.tensor_scalar(srcs[:, a_row:a_row + 2, 1, :], k_re, -1.0, None, ALU.mult)
                dve.tensor_scalar(srcs[:, b_row:b_row + 2, 0, :], k_im, -1.0, None, ALU.mult)
                chain(dve.tensor_scalar(srcs[:, b_row:b_row + 2, 1, :], k_im, -1.0, None, ALU.mult))
            dve.engine_nop().then_inc(s_srcs, 1)

            dve.wait_ge(s_turned, 2)
            for c in range(5):
                src = turned[:, (2 if c == 0 else 0):(4 if c == 0 else 2), :].rearrange("p a h -> p (a h)")
                for b in range(8):
                    ins = dve.tensor_scalar(tab[:, 8 * c + b, :], src, float(b if c == 0 else 8 * (c - 1) + b),
                                            phase[:, 0:1], ALU.mult, ALU.add)
                chain(ins)
                part = tab[:, 8 * c:8 * c + 8, :]
                chain(dve.tensor_scalar(whole[:, c % 2], part, MAGIC, MAGIC, ALU.add, ALU.subtract))
                dve.tensor_tensor(part, part, whole[:, c % 2], ALU.subtract).then_inc(s_frac, 1)
            for c in range(5):
                dve.wait_ge(s_sine, c + 1)
                dve.wait_ge(s_mod, 8 * c + 8)
                part = tab[:, 8 * c:8 * c + 8, :]
                dve.tensor_tensor(part, part, mod[:, 8 * c:8 * c + 8, :], ALU.mult).then_inc(s_tab, 1)
            dve.wait_ge(s_swap, 1)
            dve.wait_ge(s_tab, 5)
            for c in range(2):
                k_b = turned[:, 10 + 2 * c:12 + 2 * c, :].rearrange("p a h -> p (a h)")
                chain(dve.tensor_tensor(g_b[:, c, :, :], p_turn[:, :, :].rearrange("p i (a h) -> p (i a) h", a=2),
                                        k_b.unsqueeze(1).to_broadcast([P, HIGH, 2 * P]), ALU.mult))
                dve.wait_ge(s_ga, c + 1)
                dve.tensor_tensor(g_b[:, c, :, :], g_b[:, c, :, :], g_a[:, c, :, :], ALU.add).then_inc(s_g, 1)

            dve.wait_ge(s_rows, 1)
            v_view = g32[:, :, :].rearrange("p (e x) (d a b) -> p e x d a b", e=2, d=2, a=HIGH)
            for c in range(2):
                for a in range(2):
                    dst = v_view[:, :, a, c, :, :].rearrange("p e a b -> p a e b")
                    if c == 0:
                        dst = dst[:, ::-1, :, ::-1]
                    dve.tensor_copy(dst, p_rows[:, c, :, 64 * a:64 * a + 64].rearrange("p a (e b) -> p a e b", e=2)
                                    ).then_inc(s_g32, 1)
            dve.wait_ge(s_l1, 4)
            chain(dve.tensor_scalar(l1[:, :], l1[:, :], TINY, None, ALU.max))
            chain(dve.reciprocal(rl1[:, :], l1[:, :]))
            chain(dve.tensor_scalar(rl1[:, :], rl1[:, :], T_SCALE, None, ALU.mult))
            l1_v = l1[:, :].rearrange("p (e x) -> p x e", e=2)
            dve.scalar_tensor_tensor(yf[:, :], l1_v[:, 0, :], Y_SCALE, l1_v[:, 1, :], ALU.mult, ALU.mult
                                     ).then_inc(s_v16, 1)
            for r in range(4):
                dve.tensor_scalar(v16[:, r, 0, :], g32[:, r, :], rl1[:, r:r + 1], None, ALU.mult
                                  ).then_inc(s_v16, 1)
            for r in range(4):
                dve.wait_ge(s_v16, r + 2)
                dve.scalar_tensor_tensor(v16[:, r, 1, :], g32[:, r, :], rl1[:, r:r + 1], v16[:, r, 0, :],
                                         ALU.mult, ALU.subtract).then_inc(s_v16, 1)
            dve.wait_ge(s_vout, 32)
            dve.engine_nop().then_inc(y_free, 2)

            def step(it, j):
                if exists(it, j + STAT_LEAD):
                    jj = j + STAT_LEAD
                    v, k, c = jj // 2 % 4, jj // 2 % 2, 2 * (jj % 2)
                    if c == 0:
                        dve.wait_ge(x_loaded[v], it * 16 + 16 * (jj // BODY) + 16)
                    for i in range(2):
                        dve.bn_stats(bst[:, k, c + i, :], x_sb[:, v, c + i, :]).then_inc(bn_done, 1)
                    if c == 2:
                        dve.wait_ge(bn_done, it * (2 * BODY) + 2 * jj + 2)
                        dve.nop(nofuse=True)
                        dve.bn_aggr(mv[:, k, :], bst[:, k].rearrange("p c s -> p (c s)")).then_inc(agg_done, 1)
                if exists(it, j + 1):
                    k = (j + 1) % 2
                    dve.wait_ge(zh_done, it * BODY + j + 2)
                    z_v = z_ps[:, k].rearrange("p i (a r t) -> p (i a) t r", a=2, t=2)
                    for s in range(2):
                        ins = dve.scalar_tensor_tensor(zl[:, k, :, s, :], z_v[:, :, 1 - s, ::-1], Z_SCALE,
                                                       zh[:, k, :, s, :], ALU.mult, ALU.subtract)
                    ins.then_inc(zl_done, 1)
                if j % 2 and exists(it, j + CHAIN_LEAD):
                    k = (j + CHAIN_LEAD) // 2 % 2
                    dve.wait_ge(sd_done, it * 4 + (j + CHAIN_LEAD) // 2 + 1)
                    dve.reciprocal(r0[:, k:k + 1], sd[:, k:k + 1]).then_inc(rec_done, 1)
                if exists(it, j):
                    v = j // 2 % 4
                    dve.wait_ge(t_done, it * BODY + j + 1)
                    for i in range(2):
                        c = 2 * (j % 2) + i
                        t_v = t_sb[:, v, c, :].rearrange("p (s w) -> p s w", s=2)
                        y_v = y_ps[:, i, :].rearrange("p (s w) -> p s w", s=2)[:, :, ::-1]
                        dve.wait_ge(s2_done, it * (2 * BODY) + 2 * j + i + 1)
                        dve.scalar_tensor_tensor(t_v, y_v, coef[:, v, 2 + 2 * GC + c:3 + 2 * GC + c], t_v,
                                                 ALU.mult, ALU.add).then_inc(y_free, 1)

            run_steps(dve, step)

    return nc


_INS = ["x", "L0_conv_D", "L0_conv_A_re0", "L0_conv_A_re1", "L0_conv_A_im0", "L0_conv_A_im1",
        "L0_conv_C_re0", "L0_conv_C_re1", "L0_conv_C_im0", "L0_conv_C_im1",
        "L0_conv_log_dt0", "L0_conv_log_dt1"]


def kernel(**inputs):
    import numpy as np
    import concourse.bacc as bacc
    from concourse.bass_utils import run_bass_kernel_spmd

    nc = bacc.Bacc("TRN2", target_bir_lowering=False, num_devices=1)
    arrays, args = {}, []
    for name in _INS:
        a = np.ascontiguousarray(inputs[name])
        arrays[f"in_{name}"] = a
        args.append(nc.dram_tensor(f"in_{name}", a.shape, mybir.dt.from_np(a.dtype), kind="ExternalInput").ap())
    out = nc.dram_tensor("out", (B, C, L, L), F32, kind="ExternalOutput").ap()
    x, d, ar0, ar1, ai0, ai1, cr0, cr1, ci0, ci1, l0, l1 = args
    conv_block(nc, x, d.rearrange("o h -> (o h)"), (ar0, ar1), (ai0, ai1), (cr0, cr1), (ci0, ci1), (l0, l1), out)
    result = run_bass_kernel_spmd(nc, [arrays], core_ids=[0])
    return result.results[0]["out"]
```

```python
import math
from contextlib import ExitStack

import concourse.bass as bass
from concourse import mybir

ALU = mybir.AluOpType
ACT = mybir.ActivationFunctionType
AX = mybir.AxisListType
F32 = mybir.dt.float32
F16 = mybir.dt.float16
I32 = mybir.dt.int32

P = 128
B, C, L = 2, 128, 256
N = 64
GC = 4
G = C // GC
UNITS = G * B
PAIRS = UNITS * 2
LOW, HIGH = 32, 8
U_SCALE = 64.0
T_SCALE = float(2 ** 15)
Z_SCALE = 2.0 ** -15
Y_SCALE = 1.0 / (U_SCALE * T_SCALE * Z_SCALE * T_SCALE)
GN_EPS = 1e-5
TINY = 1e-30
MAGIC = 1.5 * 2 ** 23
TWO_PI = 2.0 * math.pi
TP1 = 6.28125
TP2 = float(round((TWO_PI - TP1) * 2 ** 22) / 2 ** 22)
TP3 = TWO_PI - TP1 - TP2
LN2_HI = 0.693359375
LN2_LO = math.log(2.0) - LN2_HI
SPLIT_LEAD = 3
CHAIN_LEAD = 5
STAT_LEAD = 7
BODY = 8
W_COLS = L + 2


def conv_block(nc, x, D, A_re, A_im, C_re, C_im, log_dt, out):
    x_v = x.rearrange("b (g c) (p s) w -> b g p c (s w)", c=GC, s=2)
    out_v = out.rearrange("b (g c) (p s) w -> b g p c (s w)", c=GC, s=2)
    v_dram = nc.dram_tensor("v_rows", [C, 4, 2 * L], F16, kind="Internal")
    y_dram = nc.dram_tensor("y_factor", [2, C // 2], F32, kind="Internal")

    ctx = ExitStack()
    with ctx:
        def sb(name, shape, dt=F32, where=ctx):
            return where.enter_context(nc.sbuf_tensor(name, shape, dt))

        def pb(name, shape, where=ctx):
            return where.enter_context(nc.psum_tensor(name, shape, F32))

        def sem(name):
            return ctx.enter_context(nc.semaphore(name))

        x_sb = sb("x_sb", [P, 4, GC, 2 * L])
        W = sb("W", [P, 2, GC * 4, W_COLS], F16)
        d_bc = sb("d_bc", [P, C])
        y_bc = sb("y_bc", [P, C])
        ones_neg = sb("ones_neg", [P, P])
        ones_pos = sb("ones_pos", [P, P])
        eps_gn = sb("eps_gn", [P, 1])
        bst = sb("bst", [P, 2, GC, 6])
        mv = sb("mv", [P, 2, 2])
        negm = sb("negm", [P, 2])
        dev = sb("dev", [P, 2, 2])
        ve = sb("ve", [P, 2])
        sd = sb("sd", [P, 2])
        r0 = sb("r0", [P, 2])
        nw = sb("nw", [P, 2, 4])
        d_unit = sb("d_unit", [P, 2, GC])
        coef = sb("coef", [P, 4, 2 + 2 * GC])
        y_unit = sb("y_unit", [P, 4, GC])
        turned = sb("turned", [P, 14, P])
        ident = sb("ident", [P, P])
        swap = sb("swap", [P, P])
        phase = sb("phase", [P, 1])

        gen = ExitStack()
        whole = sb("whole", [P, 2, HIGH, 2 * P], where=gen)
        mod_hi = sb("mod_hi", [P, HIGH, 2 * P], where=gen)
        srcs = sb("srcs", [P, 14, 2, N], where=gen)
        a_in = sb("a_in", [P, 2, 2, N], where=gen)
        c_in = sb("c_in", [P, 2, 2, 2, N], where=gen)
        ldt = sb("ldt", [P, 2], where=gen)
        dt = sb("dt", [P, 2], where=gen)
        dt_pow = sb("dt_pow", [P, 2], where=gen)
        xz = sb("xz", [P, 2 * N], where=gen)
        th = sb("th", [P, 2, 2 * N], where=gen)
        tau = sb("tau", [P, 2, 2 * N], where=gen)
        turns = sb("turns", [P, 2, 2 * N], where=gen)
        em = sb("em", [P, 2 * N], where=gen)
        ep = sb("ep", [P, 2 * N], where=gen)
        sin1 = sb("sin1", [P, 2 * N], where=gen)
        sinh = sb("sinh", [P, 2 * N], where=gen)
        wk = sb("wk", [P, 3, 2 * N], where=gen)
        kw = sb("kw", [P, 12, 2 * N], where=gen)
        kc = sb("kc", [P, 6, 2, 2 * N], where=gen)
        mod_lo = sb("mod_lo", [P, LOW, 2 * P], where=gen)
        tab = sb("tab", [P, LOW + HIGH, 2 * P], where=gen)
        g_a = mod_lo[:, 0:16, :].rearrange("p (c a) h -> p c a h", c=2)
        g_b = mod_lo[:, 16:32, :].rearrange("p (c a) h -> p c a h", c=2)
        gb = tab[:, 20:24, :].rearrange("p t h -> p (t h)").rearrange("p (h c a) -> p h c a", c=2, a=HIGH)
        H2 = C // 2
        g32 = tab[0:H2, 0:8, :].rearrange("p t h -> p (t h)").rearrange("p (r m) -> p r m", r=4)
        v16 = tab[0:H2, 8:16, :].rearrange("p t h -> p (t h)").bitcast(F16).rearrange(
            "p (r l m) -> p r l m", r=4, l=2)
        gabs = tab[0:H2, 16:18, :].rearrange("p t h -> p (t h)")
        l1 = sb("l1", [H2, 4], where=gen)
        rl1 = sb("rl1", [H2, 4], where=gen)
        yf = sb("yf", [H2, 2], where=gen)
        gen.close()

        u_sb = sb("u_sb", [P, 4, 4, 2, P])
        xh = sb("xh", [P, 4, 4, 2, P], F16)
        xl = sb("xl", [P, 4, 4, 2, P], F16)
        t_sb = sb("t_sb", [P, 4, GC, 2 * L])
        zh = sb("zh", [P, 2, 4, 2, P], F16)
        zl = sb("zl", [P, 2, 4, 2, P], F16)

        genp = ExitStack()
        p_turn = pb("p_turn", [P, 4, 512], where=genp)
        p_mode = pb("p_mode", [P, C // 2, 2 * HIGH], where=genp)
        genp.close()
        genq = ExitStack()
        p_rows = pb("p_rows", [C // 2, 2, HIGH, P], where=genq)
        genq.close()
        z_ps = pb("z_ps", [P, 2, 2, 512])
        y_ps = pb("y_ps", [P, 2, 512])
        st_ps = pb("st_ps", [P, 512])

        s_in = sem("params_loaded")
        s_dbc = sem("d_broadcast")
        s_const = sem("constants_ready")
        s_phase = sem("phase_ready")
        s_v = sem("vector_chain")
        s_tau = sem("tau_ready")
        s_em = sem("em_ready")
        s_k = sem("mode_factor_chain")
        s_den = sem("denominator_ready")
        s_rden = sem("reciprocal_ready")
        s_sin = sem("mode_sines_ready")
        s_srcs = sem("srcs_ready")
        s_turn = sem("turned_in_psum")
        s_turned = sem("turned_in_sbuf")
        s_mod = sem("moduli_ready")
        s_turns = sem("turns_ready")
        s_whole = sem("whole_turns_ready")
        s_frac = sem("fractions_ready")
        s_sine = sem("sines_ready")
        s_tab = sem("tables_ready")
        s_fpool = sem("pool_fractions_ready")
        s_swap = sem("exchanged_in_psum")
        s_ga = sem("g_a_ready")
        s_g = sem("g_ready")
        s_mode = sem("mode_sums_in_psum")
        s_gb = sem("mode_sums_in_sbuf")
        s_rows = sem("rows_in_psum")
        s_g32 = sem("rows_in_sbuf")
        s_hi = sem("v_hi_ready")
        s_l1 = sem("absolute_sums_ready")
        s_v16 = sem("v_rows_ready")
        s_vout = sem("v_rows_stored")
        s_ybc = sem("y_factor_broadcast")

        x_loaded = [sem(f"x_loaded{i}") for i in range(4)]
        w_loaded = [sem(f"w_loaded{i}") for i in range(2)]
        stored = [sem(f"stored{i}") for i in range(4)]
        bn_done = sem("bn_done")
        agg_done = sem("agg_done")
        mean_ps = sem("mean_ps")
        negm_done = sem("negm_done")
        dev_done = sem("dev_done")
        var_ps = sem("var_ps")
        ve_done = sem("ve_done")
        sd_done = sem("sd_done")
        rec_done = sem("rec_done")
        nw_done = sem("newton_chain")
        du_done = sem("d_unit_done")
        coef_done = sem("coef_done")
        y_done = sem("y_unit_done")
        u_done = sem("u_done")
        xh_done = sem("xh_done")
        xl_done = sem("xl_done")
        t_done = sem("t_done")
        s1_done = sem("first_product_done")
        zh_done = sem("zh_done")
        zl_done = sem("zl_done")
        s2_done = sem("second_product_done")
        y_free = sem("y_banks_free")

        block = ctx.enter_context(nc.Block())

        TURNS = PAIRS // BODY

        def exists(it, j):
            return not isinstance(it, int) or 0 <= BODY * it + j < PAIRS

        def least(value):
            return max(value, 0) if isinstance(value, int) else value

        def run_steps(eng, step):
            for j in range(-1, BODY):
                step(0, j)
            with eng.Fori(1, TURNS - 1) as it:
                for j in range(BODY):
                    step(it, j)
            for j in range(BODY):
                step(TURNS - 1, j)

        @block.sync
        def _(sp):
            with nc.allow_non_contiguous_dma(reason="two numbers per channel"):
                for a in range(2):
                    sp.dma_start(ldt[:, a:a + 1], log_dt[a].rearrange("(h o) -> h o", o=1)).then_inc(s_in, 16)
            for a in range(2):
                sp.dma_start(a_in[:, 0, a, :], A_re[a]).then_inc(s_in, 16)
                sp.dma_start(a_in[:, 1, a, :], A_im[a]).then_inc(s_in, 16)
            for a in range(2):
                sp.dma_start(c_in[:, 0, :, a, :], C_re[a].rearrange("c h n -> h c n")).then_inc(s_in, 16)
                sp.dma_start(c_in[:, 1, :, a, :], C_im[a].rearrange("c h n -> h c n")).then_inc(s_in, 16)
            sp.dma_start(d_bc[:, :], D.partition_broadcast(P)).then_inc(s_dbc, 16)

            def load_x(v, g):
                sp.dma_start(x_sb[:, v, :, :], x_v[v % 2, g]).then_inc(x_loaded[v], 16)

            def load_w(slot, g):
                rows = bass.AP(v_dram, g * (GC * 4 * 2 * L), [[2, P], [2 * L, GC * 4], [1, W_COLS]])
                sp.dma_start(W[:, slot, :, :], rows).then_inc(w_loaded[slot], 16)

            for v in range(4):
                load_x(v, v // 2)
            sp.wait_ge(s_v16, 5)
            sp.dma_start(v_dram.ap().rearrange("(e h) r m -> h e (r m)", e=2),
                         v16[:, :, :, :].rearrange("h (e a) l m -> h e (a l m)", e=2)).then_inc(s_vout, 16)
            with nc.allow_non_contiguous_dma(reason="one number per channel"):
                sp.dma_start(y_dram.ap().rearrange("e h -> h e"), yf[:, :]).then_inc(s_vout, 16)
            sp.wait_ge(s_vout, 32)
            load_w(0, 0)
            sp.dma_start(y_bc[:, :], y_dram.ap().rearrange("e h -> (e h)").partition_broadcast(P)
                         ).then_inc(s_ybc, 16)
            load_w(1, 1)

            def store(it, v):
                sp.wait_ge(y_free, it * (2 * BODY) + 4 * v + 6)
                sp.dma_start(out_v[v % 2, it * 2 + v // 2], t_sb[:, v % 4, :, :]).then_inc(stored[v % 4], 16)

            def unit(it, v, first, last):
                if not last:
                    sp.wait_ge(u_done, it * BODY + 2 * v + 2)
                    sp.wait_ge(t_done, it * BODY + 2 * v + 2)
                    load_x(v, it * 2 + 2 + v // 2)
                if v or not first:
                    store(it, v - 1)
                if v % 2 == 0 and not (first and v == 0) and not (last and v == 2):
                    sp.wait_ge(s2_done, it * (2 * BODY) + 4 * v)
                    load_w((v // 2 + 1) % 2, it * 2 + v // 2 + 1)

            for v in range(4):
                unit(0, v, True, False)
            with sp.Fori(1, TURNS - 1) as it:
                for v in range(4):
                    unit(it, v, False, False)
            for v in range(4):
                unit(TURNS - 1, v, False, True)
            store(TURNS - 1, 3)
            for v in range(4):
                sp.wait_ge(stored[v], 16 * TURNS)

        @block.gpsimd
        def _(pool):
            pool.memset(ident[:, :], 0.0).then_inc(s_const, 1)
            pool.memset(ones_neg[:, :], -1.0 / P).then_inc(s_const, 1)
            pool.memset(ones_pos[:, :], 1.0 / P).then_inc(s_const, 1)
            pool.memset(eps_gn[:, :], GN_EPS).then_inc(s_const, 1)
            pool.wait_ge(s_const, 4)
            pool.affine_select(out=ident[:, :], in_=ident[:, :], compare_op=ALU.not_equal, fill=1.0,
                               base=0, pattern=[[-1, P]], channel_multiplier=1).then_inc(s_const, 1)
            pool.wait_ge(s_const, 5)
            pool.tensor_copy(swap[:, 0:N], ident[:, N:P]).then_inc(s_const, 1)
            pool.tensor_copy(swap[:, N:P], ident[:, 0:N]).then_inc(s_const, 1)

            count = [0]

            def after(*instructions):
                for ins in instructions:
                    ins.then_inc(s_k, 1)
                count[0] += len(instructions)
                pool.wait_ge(s_k, count[0])

            def tt(out, a, b, op):
                return pool.tensor_tensor(out, a, b, op)

            k = [kw[:, i, :] for i in range(12)]
            a_re = a_in[:, 0].rearrange("p a n -> p (a n)")
            a_im = a_in[:, 1].rearrange("p a n -> p (a n)")
            pool.wait_ge(s_in, 160)
            after(tt(k[0], a_re, a_re, ALU.mult), tt(k[1], a_im, a_im, ALU.mult))
            tt(k[2], k[0], k[1], ALU.add).then_inc(s_den, 1)
            pool.wait_ge(s_sin, 1)
            after(tt(k[3], sinh[:, :], sinh[:, :], ALU.mult))
            after(pool.tensor_scalar(k[3], k[3], -2.0, 0.0, ALU.mult, ALU.add))
            pool.wait_ge(s_em, 2)
            after(tt(k[4], ep[:, :], k[3], ALU.mult), tt(k[5], ep[:, :], sin1[:, :], ALU.mult))
            after(tt(k[4], k[4], em[:, :], ALU.add))
            after(tt(k[6], k[4], a_re, ALU.mult), tt(k[7], k[5], a_im, ALU.mult),
                  tt(k[8], k[5], a_re, ALU.mult), tt(k[9], k[4], a_im, ALU.mult))
            after(tt(k[6], k[6], k[7], ALU.add), tt(k[8], k[8], k[9], ALU.subtract))
            pool.wait_ge(s_rden, 1)
            after(tt(k[10], k[6], k[2], ALU.mult), tt(k[11], k[8], k[2], ALU.mult))
            after(pool.tensor_scalar(k[10], k[10], 2.0, 0.0, ALU.mult, ALU.add),
                  pool.tensor_scalar(k[11], k[11], 2.0, 0.0, ALU.mult, ALU.add))
            c_re = c_in[:, 0].rearrange("p c a n -> p c (a n)")
            c_im = c_in[:, 1].rearrange("p c a n -> p c (a n)")
            q_re = k[10].unsqueeze(1).to_broadcast([P, 2, 2 * N])
            q_im = k[11].unsqueeze(1).to_broadcast([P, 2, 2 * N])
            after(tt(kc[:, 0], c_re, q_re, ALU.mult), tt(kc[:, 1], c_im, q_im, ALU.mult),
                  tt(kc[:, 2], c_re, q_im, ALU.mult), tt(kc[:, 3], c_im, q_re, ALU.mult))
            after(tt(kc[:, 4], kc[:, 0], kc[:, 1], ALU.subtract), tt(kc[:, 5], kc[:, 2], kc[:, 3], ALU.add))
            k_re = kc[:, 4].rearrange("p c (a n) -> p (c a) n", a=2)
            k_im = kc[:, 5].rearrange("p c (a n) -> p (c a) n", a=2)
            after(pool.tensor_copy(srcs[:, 6:10, 0, :], k_re),
                  pool.tensor_scalar(srcs[:, 6:10, 1, :], k_re, -1.0, 0.0, ALU.mult, ALU.add),
                  pool.tensor_scalar(srcs[:, 10:14, 0, :], k_im, -1.0, 0.0, ALU.mult, ALU.add),
                  pool.tensor_scalar(srcs[:, 10:14, 1, :], k_im, -1.0, 0.0, ALU.mult, ALU.add))
            pool.engine_nop().then_inc(s_srcs, 1)

            for c in (1, 2):
                pool.wait_ge(s_whole, c)
                part = tab[:, 8 * c:8 * c + 8, :]
                tt(part, part, whole[:, c % 2], ALU.subtract).then_inc(s_fpool, 1)

            pool.wait_ge(s_turned, 5)
            pool.wait_ge(s_tab, 4)
            for c in range(2):
                k_a = turned[:, 6 + 2 * c:8 + 2 * c, :].rearrange("p a h -> p (a h)")
                tt(g_a[:, c, :, :], tab[:, 0:HIGH, :],
                   k_a.unsqueeze(1).to_broadcast([P, HIGH, 2 * P]), ALU.mult).then_inc(s_ga, 1)
            pool.wait_ge(s_dbc, 16)

            def newton(it, v, dit):
                k = v % 2
                n = it * 4 + (4 * dit + v)
                g = it * 2 + (2 * dit + v // 2)
                t = [nw[:, k, i:i + 1] for i in range(4)]
                m, r = negm[:, k:k + 1], t[3]
                pool.tensor_copy(d_unit[:, k, :], d_bc[:, bass.ds(g * GC, GC)]).then_inc(du_done, 1)
                pool.wait_ge(rec_done, n + 1)
                pool.tensor_tensor(t[0], r0[:, k:k + 1], r0[:, k:k + 1], ALU.mult).then_inc(nw_done, 1)
                pool.wait_ge(nw_done, n * 4 + 1)
                pool.tensor_tensor(t[1], t[0], ve[:, k:k + 1], ALU.mult).then_inc(nw_done, 1)
                pool.wait_ge(nw_done, n * 4 + 2)
                pool.nop(nofuse=True)
                pool.tensor_scalar(t[2], t[1], -0.5, 1.5, ALU.mult, ALU.add).then_inc(nw_done, 1)
                pool.wait_ge(nw_done, n * 4 + 3)
                pool.tensor_tensor(r, t[2], r0[:, k:k + 1], ALU.mult).then_inc(nw_done, 1)
                pool.wait_ge(nw_done, n * 4 + 4)
                pool.wait_ge(du_done, n + 1)
                pool.nop(nofuse=True)
                pool.tensor_scalar(coef[:, v, 0:1], r, U_SCALE, None, ALU.mult).then_inc(coef_done, 1)
                pool.tensor_scalar(coef[:, v, 1:2], r, m, U_SCALE, ALU.mult, ALU.mult).then_inc(coef_done, 1)
                pool.tensor_scalar(coef[:, v, 2:2 + GC], d_unit[:, k, :], r, 1.0,
                                   ALU.mult, ALU.add).then_inc(coef_done, 1)
                pool.tensor_scalar(coef[:, v, 2 + GC:2 + 2 * GC], d_unit[:, k, :], r, m,
                                   ALU.mult, ALU.mult).then_inc(coef_done, 1)

            def split(it, j):
                if exists(it, j + SPLIT_LEAD):
                    jj = j + SPLIT_LEAD
                    n = it * BODY + jj
                    v = jj // 2 % 4
                    pool.wait_ge(xh_done, n + 1)
                    pool.wait_ge(s1_done, least(n - 3))
                    pool.tensor_tensor(xl[:, jj % 4], u_sb[:, jj % 4], xh[:, jj % 4], ALU.subtract
                                       ).then_inc(xl_done, 1)
                    pool.wait_ge(stored[v], least(it * 16 + 16 * (jj // BODY)))
                    pool.nop(nofuse=True)
                    for c in (2 * (jj % 2), 2 * (jj % 2) + 1):
                        ins = pool.tensor_scalar(t_sb[:, v, c, :], x_sb[:, v, c, :], coef[:, v, 2 + c:3 + c],
                                                 coef[:, v, 2 + GC + c:3 + GC + c], ALU.mult, ALU.add)
                    ins.then_inc(t_done, 1)

            def unit_scalars(it, j):
                if j % 2 and exists(it, j + CHAIN_LEAD):
                    newton(it, (j + CHAIN_LEAD) // 2 % 4, (j + CHAIN_LEAD) // BODY)

            def y_scalars(it, j):
                if j % 2 and exists(it, j + 1):
                    g = it * 2 + (j + 1) // 4
                    pool.tensor_copy(y_unit[:, (j + 1) // 2 % 4, :], y_bc[:, bass.ds(g * GC, GC)]
                                     ).then_inc(y_done, 1)

            def step(it, j):
                if not (isinstance(it, int) and BODY * it + j < 0):
                    split(it, j)
                unit_scalars(it, j)
                y_scalars(it, j)

            for j in (-5, -3):
                unit_scalars(0, j)
            for j in (-3, -2, -1):
                split(0, j)
            pool.wait_ge(s_ybc, 16)
            run_steps(pool, step)

        @block.scalar
        def _(act):
            act.wait_ge(s_tau, 1)
            act.activation(sin1[:, :], tau[:, 0, :], ACT.Sin, scale=TWO_PI)
            act.activation(sinh[:, :], tau[:, 0, :], ACT.Sin, scale=math.pi).then_inc(s_sin, 1)

            def copy_turned(rows):
                for r, e in rows:
                    act.activation(turned[:, r:e, :], p_turn[:, r // 4, 128 * (r % 4):128 * (r % 4) + 128 * (e - r)]
                                   .rearrange("p (r h) -> p r h", h=P), ACT.Copy).then_inc(s_turned, 1)

            act.wait_ge(s_turn, 1)
            copy_turned(((0, 4), (4, 6)))
            act.wait_ge(s_turned, 2)
            x_t = turned[:, 4:6, :].rearrange("p a h -> p (a h)")
            for b in range(HIGH):
                act.activation(mod_hi[:, b, :], x_t, ACT.Exp, scale=float(LOW * b)).then_inc(s_mod, 1)
            act.wait_ge(s_phase, 2)
            for b in range(16, LOW):
                act.activation(tab[:, HIGH + b, :], turned[:, 0:2, :].rearrange("p a h -> p (a h)"),
                               ACT.Identity, scale=float(b), bias=phase[:, 0:1]).then_inc(s_turns, 1)
            for b in range(LOW):
                act.activation(mod_lo[:, b, :], x_t, ACT.Exp, scale=float(b)).then_inc(s_mod, 1)
            act.wait_ge(s_turn, 2)
            copy_turned(((6, 8), (8, 12), (12, 14)))
            for c in (0, 1, 3, 2, 4):
                if c in (1, 2):
                    act.wait_ge(s_fpool, c)
                else:
                    act.wait_ge(s_frac, 1 + c // 2)
                part = tab[:, 8 * c:8 * c + 8, :]
                act.activation(part, part, ACT.Sin, scale=TWO_PI).then_inc(s_sine, 1)

            def mean_and_deviation(it, j):
                if j % 2 and exists(it, j + CHAIN_LEAD):
                    k = (j + CHAIN_LEAD) // 2 % 2
                    n = it * 4 + (j + CHAIN_LEAD) // 2
                    act.wait_ge(mean_ps, n + 1)
                    act.activation(negm[:, k:k + 1], st_ps[:, 2 * k:2 * k + 1], ACT.Copy).then_inc(negm_done, 1)
                    act.wait_ge(negm_done, n + 1)
                    act.activation(dev[:, k, 0:1], mv[:, k, 0:1], ACT.Square, bias=negm[:, k:k + 1]
                                   ).then_inc(dev_done, 1)
                    act.wait_ge(dev_done, n * 2 + 1)
                    act.activation(dev[:, k, 1:2], dev[:, k, 0:1], ACT.Identity, bias=mv[:, k, 1:2]
                                   ).then_inc(dev_done, 1)

            def split(it, j):
                if exists(it, j + SPLIT_LEAD):
                    jj = j + SPLIT_LEAD
                    m = it * BODY + jj
                    v = jj // 2 % 4
                    act.wait_ge(coef_done, it * (4 * 4) + (4 * (jj // 2) + 4))
                    act.wait_ge(xl_done, least(m - 3))
                    c = 2 * (jj % 2)
                    act.activation(u_sb[:, jj % 4],
                                   x_sb[:, v, c:c + 2, :].rearrange("p c (s q t) -> p (c s) t q", s=2, t=2),
                                   ACT.Identity, bias=coef[:, v, 1:2], scale=coef[:, v, 0:1]).then_inc(u_done, 1)
                    act.wait_ge(u_done, m + 1)
                    act.wait_ge(s1_done, least(m - 3))
                    act.activation(xh[:, jj % 4], u_sb[:, jj % 4], ACT.Copy).then_inc(xh_done, 1)

            def z_hi(it, j):
                if exists(it, j + 1):
                    m = it * BODY + j
                    z = (j + 1) % 2
                    act.wait_ge(s1_done, m + 2)
                    act.wait_ge(s2_done, least(m * 2))
                    act.activation(zh[:, z], z_ps[:, z].rearrange("p i (a r t) -> p (i a) t r", a=2, t=2)
                                   [:, :, ::-1, ::-1], ACT.Copy, scale=Z_SCALE).then_inc(zh_done, 1)

            def root(it, j):
                if j % 2 and exists(it, j + CHAIN_LEAD):
                    k = (j + CHAIN_LEAD) // 2 % 2
                    n = it * 4 + (j + CHAIN_LEAD) // 2
                    act.wait_ge(var_ps, n + 1)
                    act.activation(ve[:, k:k + 1], st_ps[:, 2 * k + 1:2 * k + 2], ACT.Identity,
                                   bias=eps_gn[:, 0:1]).then_inc(ve_done, 1)
                    act.wait_ge(ve_done, n + 1)
                    act.activation(sd[:, k:k + 1], ve[:, k:k + 1], ACT.Sqrt).then_inc(sd_done, 1)

            def step(it, j):
                mean_and_deviation(it, j)
                if not (isinstance(it, int) and BODY * it + j < 0):
                    split(it, j)
                z_hi(it, j)
                root(it, j)

            for j in (-5, -3):
                mean_and_deviation(0, j)
                root(0, j)
            for j in (-3, -2, -1):
                split(0, j)
            act.wait_ge(s_mode, 1)
            act.activation(gb, p_mode[:, :, :], ACT.Copy).then_inc(s_gb, 1)
            act.wait_ge(s_g32, 4)
            for r in range(4):
                if r:
                    act.wait_ge(s_l1, r)
                act.activation(gabs, g32[:, r, :], ACT.Abs, accum_out=l1[:, r:r + 1]).then_inc(s_l1, 1)
            act.wait_ge(s_v16, 1)
            for r in range(4):
                act.activation(v16[:, r, 0, :], g32[:, r, :], ACT.Copy, scale=rl1[:, r:r + 1]).then_inc(s_hi, 1)

            run_steps(act, step)

        @block.tensor
        def _(pe):
            def means(it, j):
                if j % 2 and exists(it, j + CHAIN_LEAD):
                    k = (j + CHAIN_LEAD) // 2 % 2
                    pe.wait_ge(agg_done, it * 4 + (j + CHAIN_LEAD) // 2 + 1)
                    pe.matmul(st_ps[:, 2 * k:2 * k + 1], ones_neg[:, :], mv[:, k, 0:1],
                              start=True, stop=True).then_inc(mean_ps, 1)

            def variances(it, j):
                if j % 2 and exists(it, j + CHAIN_LEAD):
                    k = (j + CHAIN_LEAD) // 2 % 2
                    pe.wait_ge(dev_done, it * 8 + 2 * ((j + CHAIN_LEAD) // 2) + 2)
                    pe.matmul(st_ps[:, 2 * k + 1:2 * k + 2], ones_pos[:, :], dev[:, k, 1:2],
                              start=True, stop=True).then_inc(var_ps, 1)

            def first_product(it, j):
                if exists(it, j + 1):
                    jj = j + 1
                    w = jj // 4 % 2
                    if jj % 4 == 0:
                        pe.wait_ge(w_loaded[w], it * 16 + 16 * (jj // BODY) + 16)
                    pe.wait_ge(xl_done, it * BODY + j + 2)
                    for i in range(2):
                        row = 4 * (2 * (jj % 2) + i)
                        for t in range(2):
                            n_mm = 0
                            for s in range(2):
                                for u, half in ((xh, 0), (xh, 1), (xl, 0)):
                                    ins = pe.matmul(z_ps[:, jj % 2, i, L * t:L * t + L], u[:, jj % 4, 2 * i + s, t, :],
                                                    W[:, w, row + half, s:s + L], start=n_mm == 0, stop=n_mm == 5)
                                    n_mm += 1
                    ins.then_inc(s1_done, 1)

            def second_product(it, j):
                if exists(it, j):
                    w = j // 4 % 2
                    pe.wait_ge(zl_done, it * BODY + j + 1)
                    for i in range(2):
                        row = 4 * (2 * (j % 2) + i) + 2
                        pe.wait_ge(y_free, it * (2 * BODY) + 2 * j + i + 1)
                        for s in range(2):
                            n_mm = 0
                            for t in range(2):
                                for z, half in ((zh, 0), (zh, 1), (zl, 0)):
                                    ins = pe.matmul(y_ps[:, i, L * s:L * s + L], z[:, j % 2, 2 * i + t, s, :],
                                                    W[:, w, row + half, t:t + L], start=n_mm == 0, stop=n_mm == 5)
                                    n_mm += 1
                        ins.then_inc(s2_done, 1)

            pe.wait_ge(s_const, 7)
            for i, rows in enumerate((range(6), range(6, 14))):
                pe.wait_ge(s_srcs, i + 4)
                if i == 1:
                    pe.wait_ge(s_turned, 2)
                for r in rows:
                    ins = pe.transpose(p_turn[:, r // 4, 128 * (r % 4):128 * (r % 4) + 128],
                                       srcs[:, r].rearrange("p a n -> p (a n)"), ident[:, :])
                ins.then_inc(s_turn, 1)
            pe.wait_ge(s_tab, 1)
            pe.wait_ge(s_turned, 5)
            for i in range(4):
                ins = pe.matmul(p_turn[:, i, :], swap[:, :],
                                tab[:, 2 * i:2 * i + 2, :].rearrange("p a h -> p (a h)"), start=True, stop=True)
            ins.then_inc(s_swap, 1)
            for j in (-5, -3):
                if j == -3:
                    pe.wait_ge(ve_done, 1)
                means(0, j)
                variances(0, j)
            pe.wait_ge(s_tab, 5)
            for a in range(2):
                pe.wait_ge(s_g, 2 * a + 2)
                for h in range(C):
                    q, hs = 32 * (2 * a + h // (C // 2)), h % (C // 2)
                    ins = pe.matmul(p_mode[q:q + 32, hs, :], tab[:, HIGH:, a * P + h],
                                    g_b[:, :, :, a * P + h], start=True, stop=True)
            ins.then_inc(s_mode, 1)
            pe.wait_ge(s_gb, 1)
            for c in range(2):
                for a in range(HIGH):
                    ins = pe.transpose(p_rows[:, c, a, :], gb[:, :, c, a], ident[:, :])
            ins.then_inc(s_rows, 1)
            pe.wait_ge(s_g32, 4)

            def step(it, j):
                means(it, j)
                first_product(it, j)
                variances(it, j)
                second_product(it, j)

            run_steps(pe, step)

        @block.vector
        def _(dve):
            count = [0]

            def chain(ins):
                count[0] += 1
                ins.then_inc(s_v, 1)
                dve.wait_ge(s_v, count[0])

            def exp_parts(src, res, power, w):
                k, r = w
                chain(dve.tensor_scalar(r, src, -87.0, 88.0, ALU.max, ALU.min))
                chain(dve.tensor_scalar(k, r, 1.0 / math.log(2.0), MAGIC, ALU.mult, ALU.add))
                chain(dve.tensor_scalar(k, k, MAGIC, None, ALU.subtract))
                chain(dve.scalar_tensor_tensor(r, k, -LN2_HI, r, ALU.mult, ALU.add))
                chain(dve.scalar_tensor_tensor(r, k, -LN2_LO, r, ALU.mult, ALU.add))
                chain(dve.tensor_scalar(power.bitcast(I32), k, 127.0, float(2 ** 23), ALU.add, ALU.mult))
                chain(dve.tensor_scalar(res, r, 1.0 / 5040.0, None, ALU.mult))
                for f in (720.0, 120.0, 24.0, 6.0, 2.0, 1.0):
                    chain(dve.scalar_tensor_tensor(res, res, 1.0 / f, r, ALU.add, ALU.mult))

            def sums(it, j):
                if exists(it, j + STAT_LEAD):
                    jj = j + STAT_LEAD
                    v, k, c = jj // 2 % 4, jj // 2 % 2, 2 * (jj % 2)
                    if c == 0:
                        dve.wait_ge(x_loaded[v], it * 16 + 16 * (jj // BODY) + 16)
                    for i in range(2):
                        dve.bn_stats(bst[:, k, c + i, :], x_sb[:, v, c + i, :]).then_inc(bn_done, 1)
                    if c == 2:
                        dve.wait_ge(bn_done, it * (2 * BODY) + 2 * jj + 2)
                        dve.nop(nofuse=True)
                        dve.bn_aggr(mv[:, k, :], bst[:, k].rearrange("p c s -> p (c s)")).then_inc(agg_done, 1)

            def root_reciprocal(it, j):
                if j % 2 and exists(it, j + CHAIN_LEAD):
                    k = (j + CHAIN_LEAD) // 2 % 2
                    dve.wait_ge(sd_done, it * 4 + (j + CHAIN_LEAD) // 2 + 1)
                    dve.reciprocal(r0[:, k:k + 1], sd[:, k:k + 1]).then_inc(rec_done, 1)

            w0, w1, w2 = (wk[:, i, :] for i in range(3))
            dve.memset(phase[0:N, :], 0.25).then_inc(s_phase, 1)
            dve.memset(phase[N:P, :], 0.0).then_inc(s_phase, 1)
            dve.wait_ge(s_in, 160)
            exp_parts(ldt[:, :], dt[:, :], dt_pow[:, :], (wk[:, 0, 0:2], wk[:, 1, 0:2]))
            chain(dve.scalar_tensor_tensor(dt[:, :], dt[:, :], 1.0, dt_pow[:, :], ALU.add, ALU.mult))
            for a in range(2):
                dve.tensor_scalar(xz[:, a * N:a * N + N], a_in[:, 0, a, :], dt[:, a:a + 1], None, ALU.mult)
                dve.tensor_scalar(th[:, 0, a * N:a * N + N], a_in[:, 1, a, :], dt[:, a:a + 1], None, ALU.mult)
                chain(dve.tensor_scalar(th[:, 1, a * N:a * N + N], a_in[:, 1, a, :], dt[:, a:a + 1], float(LOW),
                                        ALU.mult, ALU.mult))
            chain(dve.tensor_scalar(turns[:, :, :], th[:, :, :], 1.0 / TWO_PI, MAGIC, ALU.mult, ALU.add))
            chain(dve.tensor_scalar(turns[:, :, :], turns[:, :, :], MAGIC, None, ALU.subtract))
            chain(dve.scalar_tensor_tensor(tau[:, :, :], turns[:, :, :], -TP1, th[:, :, :], ALU.mult, ALU.add))
            chain(dve.scalar_tensor_tensor(tau[:, :, :], turns[:, :, :], -TP2, tau[:, :, :], ALU.mult, ALU.add))
            chain(dve.scalar_tensor_tensor(tau[:, :, :], turns[:, :, :], -TP3, tau[:, :, :], ALU.mult, ALU.add))
            chain(dve.tensor_scalar(tau[:, :, :], tau[:, :, :], 1.0 / TWO_PI, -0.5, ALU.mult, ALU.max))
            dve.tensor_scalar(tau[:, :, :], tau[:, :, :], 0.5, None, ALU.min).then_inc(s_tau, 1)
            dve.wait_ge(s_tau, 1)
            for h in range(2):
                dve.tensor_copy(srcs[:, 0:4, h, :], tau[:, :, :].rearrange("p l (a n) -> p (l a) n", a=2)
                                ).then_inc(s_srcs, 1)
                dve.tensor_copy(srcs[:, 4:6, h, :], xz[:, :].rearrange("p (a n) -> p a n", a=2)
                                ).then_inc(s_srcs, 1)
            exp_parts(xz[:, :], em[:, :], w2, (w0, w1))
            chain(dve.tensor_tensor(em[:, :], em[:, :], w2, ALU.mult))
            dve.tensor_tensor(ep[:, :], em[:, :], w2, ALU.add).then_inc(s_em, 1)
            chain(dve.scalar_tensor_tensor(em[:, :], w2, -1.0, em[:, :], ALU.add, ALU.add))
            dve.wait_ge(s_den, 1)
            dve.reciprocal(kw[:, 2, :], kw[:, 2, :]).then_inc(s_rden, 1)
            dve.engine_nop().then_inc(s_em, 1)

            dve.wait_ge(s_turned, 2)
            dve.wait_ge(s_phase, 2)
            for c in range(5):
                part = tab[:, 8 * c:8 * c + 8, :]
                if c < 3:
                    src = turned[:, (2 if c == 0 else 0):(4 if c == 0 else 2), :].rearrange("p a h -> p (a h)")
                    for b in range(8):
                        ins = dve.tensor_scalar(tab[:, 8 * c + b, :], src, float(b if c == 0 else 8 * (c - 1) + b),
                                                phase[:, 0:1], ALU.mult, ALU.add)
                    chain(ins)
                else:
                    dve.wait_ge(s_turns, 8 * (c - 2))
                    dve.wait_ge(s_fpool, c - 2)
                ins = dve.tensor_scalar(whole[:, c % 2], part, MAGIC, MAGIC, ALU.add, ALU.subtract)
                if c in (1, 2):
                    ins.then_inc(s_whole, 1)
                else:
                    chain(ins)
                    dve.tensor_tensor(part, part, whole[:, c % 2], ALU.subtract).then_inc(s_frac, 1)
            for j in range(-STAT_LEAD, -3):
                sums(0, j)
            for n, c in enumerate((0, 1, 3, 2, 4)):
                dve.wait_ge(s_sine, n + 1)
                dve.wait_ge(s_mod, 8 * c + 8)
                part = tab[:, 8 * c:8 * c + 8, :]
                m = mod_hi[:, :, :] if c == 0 else mod_lo[:, 8 * c - 8:8 * c, :]
                dve.tensor_tensor(part, part, m, ALU.mult).then_inc(s_tab, 1)
            root_reciprocal(0, -5)
            dve.wait_ge(s_tab, 5)
            dve.wait_ge(s_swap, 1)
            e_x = p_turn[:, :, :].rearrange("p i (b h) -> p (i b) h", b=2)
            for a in range(2):
                cols = slice(a * P, a * P + P)
                for c in range(2):
                    k_b = turned[:, 10 + 2 * c + a, :]
                    chain(dve.tensor_tensor(g_b[:, c, :, cols], e_x[:, :, cols],
                                            k_b.unsqueeze(1).to_broadcast([P, HIGH, P]), ALU.mult))
                    dve.wait_ge(s_ga, c + 1)
                    dve.tensor_tensor(g_b[:, c, :, cols], g_b[:, c, :, cols], g_a[:, c, :, cols], ALU.add
                                      ).then_inc(s_g, 1)
                if a == 0:
                    root_reciprocal(0, -3)
            sums(0, -3)
            sums(0, -2)

            dve.wait_ge(s_rows, 1)
            v_view = g32[:, :, :].rearrange("p (e x) (d a b) -> p e x d a b", e=2, d=2, a=HIGH)
            for c in range(2):
                for a in range(2):
                    dst = v_view[:, :, a, c, :, :].rearrange("p e a b -> p a e b")
                    if c == 0:
                        dst = dst[:, ::-1, :, ::-1]
                    dve.tensor_copy(dst, p_rows[:, c, :, 64 * a:64 * a + 64].rearrange("p a (e b) -> p a e b", e=2)
                                    ).then_inc(s_g32, 1)
            dve.wait_ge(s_l1, 4)
            chain(dve.tensor_scalar(l1[:, :], l1[:, :], TINY, None, ALU.max))
            chain(dve.reciprocal(rl1[:, :], l1[:, :]))
            chain(dve.tensor_scalar(rl1[:, :], rl1[:, :], T_SCALE, None, ALU.mult))
            l1_v = l1[:, :].rearrange("p (e x) -> p x e", e=2)
            dve.scalar_tensor_tensor(yf[:, :], l1_v[:, 0, :], Y_SCALE, l1_v[:, 1, :], ALU.mult, ALU.mult
                                     ).then_inc(s_v16, 1)
            for r in range(4):
                dve.wait_ge(s_hi, r + 1)
                dve.scalar_tensor_tensor(v16[:, r, 1, :], g32[:, r, :], rl1[:, r:r + 1], v16[:, r, 0, :],
                                         ALU.mult, ALU.subtract).then_inc(s_v16, 1)
            dve.wait_ge(s_vout, 32)
            dve.engine_nop().then_inc(y_free, 2)

            def z_lo(it, j):
                if exists(it, j + 1):
                    k = (j + 1) % 2
                    dve.wait_ge(zh_done, it * BODY + j + 2)
                    z_v = z_ps[:, k].rearrange("p i (a r t) -> p (i a) t r", a=2, t=2)
                    for s in range(2):
                        ins = dve.scalar_tensor_tensor(zl[:, k, :, s, :], z_v[:, :, 1 - s, ::-1], Z_SCALE,
                                                       zh[:, k, :, s, :], ALU.mult, ALU.subtract)
                    ins.then_inc(zl_done, 1)

            def results(it, j):
                if exists(it, j):
                    v = j // 2 % 4
                    dve.wait_ge(t_done, it * BODY + j + 1)
                    dve.wait_ge(y_done, it * 4 + j // 2 + 1)
                    for i in range(2):
                        c = 2 * (j % 2) + i
                        t_v = t_sb[:, v, c, :].rearrange("p (s w) -> p s w", s=2)
                        y_v = y_ps[:, i, :].rearrange("p (s w) -> p s w", s=2)[:, :, ::-1]
                        dve.wait_ge(s2_done, it * (2 * BODY) + 2 * j + i + 1)
                        dve.scalar_tensor_tensor(t_v, y_v, y_unit[:, v, c:c + 1], t_v,
                                                 ALU.mult, ALU.add).then_inc(y_free, 1)

            def step(it, j):
                sums(it, j)
                z_lo(it, j)
                root_reciprocal(it, j)
                results(it, j)

            run_steps(dve, step)

    return nc


_INS = ["x", "L0_conv_D", "L0_conv_A_re0", "L0_conv_A_re1", "L0_conv_A_im0", "L0_conv_A_im1",
        "L0_conv_C_re0", "L0_conv_C_re1", "L0_conv_C_im0", "L0_conv_C_im1",
        "L0_conv_log_dt0", "L0_conv_log_dt1"]


def kernel(**inputs):
    import numpy as np
    import concourse.bacc as bacc
    from concourse.bass_utils import run_bass_kernel_spmd

    nc = bacc.Bacc("TRN2", target_bir_lowering=False, num_devices=1)
    arrays, args = {}, []
    for name in _INS:
        a = np.ascontiguousarray(inputs[name])
        arrays[f"in_{name}"] = a
        args.append(nc.dram_tensor(f"in_{name}", a.shape, mybir.dt.from_np(a.dtype), kind="ExternalInput").ap())
    out = nc.dram_tensor("out", (B, C, L, L), F32, kind="ExternalOutput").ap()
    x, d, ar0, ar1, ai0, ai1, cr0, cr1, ci0, ci1, l0, l1 = args
    conv_block(nc, x, d.rearrange("o h -> (o h)"), (ar0, ar1), (ai0, ai1), (cr0, cr1), (ci0, ci1), (l0, l1), out)
    result = run_bass_kernel_spmd(nc, [arrays], core_ids=[0])
    return result.results[0]["out"]
```

```python
import math
from contextlib import ExitStack

import concourse.bass as bass
from concourse import mybir

ALU = mybir.AluOpType
ACT = mybir.ActivationFunctionType
AX = mybir.AxisListType
F32 = mybir.dt.float32
F16 = mybir.dt.float16
I32 = mybir.dt.int32

P = 128
B, C, L = 2, 128, 256
N = 64
GC = 4
G = C // GC
UNITS = G * B
PAIRS = UNITS * 2
LOW, HIGH = 32, 8
U_SCALE = 64.0
T_SCALE = float(2 ** 15)
Z_SCALE = 2.0 ** -15
Y_SCALE = 1.0 / (U_SCALE * T_SCALE * Z_SCALE * T_SCALE)
GN_EPS = 1e-5
TINY = 1e-30
MAGIC = 1.5 * 2 ** 23
TWO_PI = 2.0 * math.pi
TP1 = 6.28125
TP2 = float(round((TWO_PI - TP1) * 2 ** 22) / 2 ** 22)
TP3 = TWO_PI - TP1 - TP2
LN2_HI = 0.693359375
LN2_LO = math.log(2.0) - LN2_HI
SPLIT_LEAD = 3
VAR_LEAD = 4
MEAN_LEAD = 8
STAT_LEAD = 12
BODY = 16
W_COLS = L + 2


def conv_block(nc, x, D, A_re, A_im, C_re, C_im, log_dt, out):
    x_v = x.rearrange("b (g c) (p s) w -> b g p c (s w)", c=GC, s=2)
    out_v = out.rearrange("b (g c) (p s) w -> b g p c (s w)", c=GC, s=2)
    v_dram = nc.dram_tensor("v_rows", [C, 4, 2 * L], F16, kind="Internal")
    y_dram = nc.dram_tensor("y_factor", [2, C // 2], F32, kind="Internal")

    ctx = ExitStack()
    with ctx:
        def sb(name, shape, dt=F32, where=ctx):
            return where.enter_context(nc.sbuf_tensor(name, shape, dt))

        def pb(name, shape, where=ctx):
            return where.enter_context(nc.psum_tensor(name, shape, F32))

        def sem(name):
            return ctx.enter_context(nc.semaphore(name))

        x_lo = sb("x_lo", [P, 4, GC, 2 * L])
        W = sb("W", [P, 2, GC * 4, W_COLS], F16)
        d_bc = sb("d_bc", [P, C])
        y_bc = sb("y_bc", [P, C])
        ones = sb("ones", [P, P])
        eps_gn = sb("eps_gn", [P, 1])
        bst = sb("bst", [P, 2, 2, GC, 6])
        st = sb("st", [P, 2, 6])
        negm = sb("negm", [P, 2, 2])
        sq = sb("sq", [P, 2, 2])
        ve = sb("ve", [P, 2, 2])
        sd = sb("sd", [P, 2, 2])
        r0 = sb("r0", [P, 2, 2])
        nw = sb("nw", [P, 2, 10])
        d_grp = sb("d_grp", [P, 2, GC])
        u_coef = sb("u_coef", [P, 4, 2, 2])
        t_coef = sb("t_coef", [P, 4, 2, 2, GC])
        y_grp = sb("y_grp", [P, 4, GC])
        turned = sb("turned", [P, 14, P])
        ident = sb("ident", [P, P])
        swap = sb("swap", [P, P])
        phase = sb("phase", [P, 1])

        gen = ExitStack()
        whole = sb("whole", [P, 2, HIGH, 2 * P], where=gen)
        mod_hi = sb("mod_hi", [P, HIGH, 2 * P], where=gen)
        srcs = sb("srcs", [P, 14, 2, N], where=gen)
        a_in = sb("a_in", [P, 2, 2, N], where=gen)
        c_in = sb("c_in", [P, 2, 2, 2, N], where=gen)
        ldt = sb("ldt", [P, 2], where=gen)
        dt = sb("dt", [P, 2], where=gen)
        dt_pow = sb("dt_pow", [P, 2], where=gen)
        xz = sb("xz", [P, 2 * N], where=gen)
        th = sb("th", [P, 2, 2 * N], where=gen)
        tau = sb("tau", [P, 2, 2 * N], where=gen)
        turns = sb("turns", [P, 2, 2 * N], where=gen)
        em = sb("em", [P, 2 * N], where=gen)
        ep = sb("ep", [P, 2 * N], where=gen)
        sin1 = sb("sin1", [P, 2 * N], where=gen)
        sinh = sb("sinh", [P, 2 * N], where=gen)
        wk = sb("wk", [P, 3, 2 * N], where=gen)
        kw = sb("kw", [P, 12, 2 * N], where=gen)
        kc = sb("kc", [P, 6, 2, 2 * N], where=gen)
        mod_lo = sb("mod_lo", [P, LOW, 2 * P], where=gen)
        tab = sb("tab", [P, LOW + HIGH, 2 * P], where=gen)
        g_a = whole
        g_b = mod_lo[:, 16:32, :].rearrange("p (c a) h -> p c a h", c=2)
        gb = whole[:, 0, 0:4, :].rearrange("p t h -> p (t h)").rearrange("p (h c a) -> p h c a", c=2, a=HIGH)
        H2 = C // 2
        g32 = tab[0:H2, 24:32, :].rearrange("p t h -> p (t h)").rearrange("p (r m) -> p r m", r=4)
        v16 = tab[0:H2, 32:40, :].rearrange("p t h -> p (t h)").bitcast(F16).rearrange(
            "p (r l m) -> p r l m", r=4, l=2)
        gabs = tab[0:H2, 18:20, :].rearrange("p t h -> p (t h)")
        l1 = sb("l1", [H2, 4], where=gen)
        rl1 = sb("rl1", [H2, 4], where=gen)
        yf = sb("yf", [H2, 2], where=gen)
        gen.close()

        u_sb = sb("u_sb", [P, 4, 4, 2, P])
        xh = sb("xh", [P, 4, 4, 2, P], F16)
        xl = sb("xl", [P, 4, 4, 2, P], F16)
        t_sb = sb("t_sb", [P, 4, GC, 2 * L])
        x_hi = sb("x_hi", [P, 4, GC, 2 * L])
        zh = sb("zh", [P, 2, 4, 2, P], F16)
        zl = sb("zl", [P, 2, 4, 2, P], F16)

        genp = ExitStack()
        p_turn = pb("p_turn", [P, 4, 512], where=genp)
        p_mode = pb("p_mode", [P, C // 2, 2 * HIGH], where=genp)
        p_kturn = p_mode[:, :, :].rearrange("p h m -> p (h m)")
        genp.close()
        genq = ExitStack()
        p_rows = pb("p_rows", [C // 2, 2, HIGH, P], where=genq)
        genq.close()
        z_ps = pb("z_ps", [P, 2, 2, 512])
        y_ps = pb("y_ps", [P, 2, 512])
        st_ps = pb("st_ps", [P, 512])
        warm_ps = pb("warm_ps", [P, 512])

        s_ldt = sem("log_dt_loaded")
        s_a = sem("a_loaded")
        s_c = sem("c_loaded")
        s_dbc = sem("d_broadcast")
        s_const = sem("constants_ready")
        s_phase = sem("phase_ready")
        s_st = sem("first_squares_cleared")
        s_v = sem("vector_chain")
        s_tau = sem("tau_ready")
        s_em = sem("em_ready")
        s_k = sem("mode_factor_chain")
        s_den = sem("denominator_ready")
        s_rden = sem("reciprocal_ready")
        s_sin = sem("mode_sines_ready")
        s_srcs = sem("srcs_ready")
        s_ksrc = sem("k_sources_ready")
        s_turn = sem("turned_in_psum")
        s_turned = sem("turned_in_sbuf")
        s_kturn = sem("k_turned_in_psum")
        s_kturned = sem("k_turned_in_sbuf")
        s_mod = sem("moduli_ready")
        s_turns = sem("scalar_turns_ready")
        s_pturns = sem("pool_turns_ready")
        s_whole = sem("whole_turns_ready")
        s_frac = sem("fractions_ready")
        s_sine = sem("sines_ready")
        s_tab = [sem(f"tables_ready_axis{a}") for a in range(2)]
        s_ptab = sem("pool_tables_ready")
        s_fpool = sem("pool_fractions_ready")
        s_swap = sem("exchanged_in_psum")
        s_ga = sem("g_a_ready")
        s_g = sem("g_ready")
        s_mode = sem("mode_sums_in_psum")
        s_gb = sem("mode_sums_in_sbuf")
        s_rows = sem("rows_in_psum")
        s_g32 = sem("rows_in_sbuf")
        s_g32b = sem("backward_rows_in_sbuf")
        s_hi = sem("v_hi_ready")
        s_l1 = sem("absolute_sums_ready")
        s_l1v = sem("vector_absolute_sums_ready")
        s_rl1 = sem("scales_of_v_ready")
        s_yf = sem("y_factor_ready")
        s_v16 = sem("v_rows_ready")
        s_vout = [sem(f"v_rows_stored{e}") for e in range(2)]
        s_yout = sem("y_factor_stored")
        s_wfirst = sem("first_toeplitz_half_loaded")
        s_mean1 = sem("group1_means_in_psum")
        s_ybc = sem("y_factor_broadcast")

        x_loaded = [sem(f"x_loaded{i}") for i in range(8)]
        w_loaded = [sem(f"w_loaded{i}") for i in range(2)]
        stored = [sem(f"stored{i}") for i in range(4)]
        bn_done = sem("bn_done")
        agg_done = sem("agg_done")
        stat_ps = sem("partition_sums_in_psum")
        negm_done = sem("negm_done")
        dev_done = sem("dev_done")
        ve_done = sem("ve_done")
        sd_done = sem("sd_done")
        rec_done = sem("rec_done")
        nw_done = sem("newton_chain")
        dg_done = sem("d_group_done")
        coef_done = sem("coef_done")
        y_done = sem("y_group_done")
        u_done = sem("u_done")
        xh_done = sem("xh_done")
        xl_done = sem("xl_done")
        t_done = sem("t_done")
        s1_done = sem("first_product_done")
        zh_done = sem("zh_done")
        zl_done = sem("zl_done")
        s2_done = sem("second_product_done")
        y_free = sem("y_banks_free")

        block = ctx.enter_context(nc.Block())

        TURNS = PAIRS // BODY

        def exists(it, j):
            return not isinstance(it, int) or 0 <= BODY * it + j < PAIRS

        def least(value):
            return max(value, 0) if isinstance(value, int) else value

        def x_tile(v):
            return x_lo[:, v] if v < 4 else x_hi[:, v - 4]

        def run_steps(eng, step):
            for j in range(-1, BODY):
                step(0, j)
            with eng.Fori(1, TURNS - 1) as it:
                for j in range(BODY):
                    step(it, j)
            for j in range(BODY):
                step(TURNS - 1, j)

        v_view = g32[:, :, :].rearrange("p (e x) (d a b) -> p e x d a b", e=2, d=2, a=HIGH)

        def row_parts(c):
            for a in range(2):
                dst = v_view[:, :, a, c, :, :].rearrange("p e a b -> p a e b")
                if c == 0:
                    dst = dst[:, ::-1, :, ::-1]
                yield dst, p_rows[:, c, :, 64 * a:64 * a + 64].rearrange("p a (e b) -> p a e b", e=2)

        @block.sync
        def _(sp):
            with nc.allow_non_contiguous_dma(reason="two numbers per channel"):
                for a in range(2):
                    sp.dma_start(ldt[:, a:a + 1], log_dt[a].rearrange("(h o) -> h o", o=1)).then_inc(s_ldt, 16)
            for a in range(2):
                sp.dma_start(a_in[:, 0, a, :], A_re[a]).then_inc(s_a, 16)
                sp.dma_start(a_in[:, 1, a, :], A_im[a]).then_inc(s_a, 16)
            for a in range(2):
                sp.dma_start(c_in[:, 0, :, a, :], C_re[a].rearrange("c h n -> h c n")).then_inc(s_c, 16)
                sp.dma_start(c_in[:, 1, :, a, :], C_im[a].rearrange("c h n -> h c n")).then_inc(s_c, 16)

            def load_x(v, g):
                sp.dma_start(x_tile(v), x_v[v % 2, g]).then_inc(x_loaded[v], 16)

            def w_rows(g, first, last):
                return bass.AP(v_dram, (g * GC * 4 + first) * (2 * L),
                               [[2, P], [2 * L, last - first], [1, W_COLS]])

            def load_w(slot, g):
                sp.dma_start(W[:, slot, :, :], w_rows(g, 0, GC * 4)).then_inc(w_loaded[slot], 16)

            load_x(0, 0)
            sp.dma_start(d_bc[:, :], D.partition_broadcast(P)).then_inc(s_dbc, 16)
            for v in range(1, 4):
                load_x(v, v // 2)
            sp.wait_ge(s_mode, 2)
            load_x(4, 2)
            load_x(5, 2)
            v_rows = v_dram.ap().rearrange("(e h) r m -> e h (r m)", e=2)
            for e in range(2):
                sp.wait_ge(s_v16, 2 * e + 2)
                sp.dma_start(v_rows[e], v16[:, 2 * e:2 * e + 2, :, :].rearrange("h a l m -> h (a l m)")
                             ).then_inc(s_vout[e], 16)
                if e == 0:
                    sp.wait_ge(s_vout[0], 16)
                    sp.dma_start(W[:, 0, 0:8, :], w_rows(0, 0, 8)).then_inc(s_wfirst, 16)
            sp.wait_ge(s_yf, 1)
            with nc.allow_non_contiguous_dma(reason="one number per channel"):
                sp.dma_start(y_dram.ap().rearrange("e h -> h e"), yf[:, :]).then_inc(s_yout, 16)
            sp.dma_start(W[:, 0, 8:16, :], w_rows(0, 8, 16)).then_inc(w_loaded[0], 16)
            sp.wait_ge(s_yout, 16)
            sp.dma_start(y_bc[:, :], y_dram.ap().rearrange("e h -> (e h)").partition_broadcast(P)
                         ).then_inc(s_ybc, 16)
            load_x(6, 3)
            load_w(1, 1)
            load_x(7, 3)
            sp.wait_ge(s_vout[1], 16)

            def store(it, v):
                sp.wait_ge(y_free, it * (2 * BODY) + 4 * v + 6)
                sp.dma_start(out_v[v % 2, it * 4 + v // 2], t_sb[:, v % 4, :, :]).then_inc(stored[v % 4], 16)

            def unit(it, v, first, last):
                if not last:
                    sp.wait_ge(u_done, it * BODY + 2 * v + 2)
                    sp.wait_ge(t_done, it * BODY + 2 * v + 2)
                    load_x(v, it * 4 + 4 + v // 2)
                if v or not first:
                    store(it, v - 1)
                if v % 2 == 0 and not (first and v == 0) and not (last and v == 6):
                    sp.wait_ge(s2_done, it * (2 * BODY) + 4 * v)
                    load_w((v // 2 + 1) % 2, it * 4 + v // 2 + 1)

            for v in range(8):
                unit(0, v, True, False)
            with sp.Fori(1, TURNS - 1) as it:
                for v in range(8):
                    unit(it, v, False, False)
            for v in range(8):
                unit(TURNS - 1, v, False, True)
            for c in (0, 2):
                sp.wait_ge(y_free, 2 * PAIRS + c)
                sp.dma_start(out_v[1, G - 1, :, c:c + 2], t_sb[:, 3, c:c + 2, :]).then_inc(stored[3], 16)
            for v in range(4):
                sp.wait_ge(stored[v], 32 * TURNS + (16 if v == 3 else 0))

        @block.gpsimd
        def _(pool):
            pool.memset(ident[:, :], 0.0).then_inc(s_const, 1)
            pool.memset(ones[:, :], 1.0 / P).then_inc(s_const, 1)
            pool.memset(eps_gn[:, :], GN_EPS).then_inc(s_const, 1)
            pool.wait_ge(s_const, 3)
            pool.affine_select(out=ident[:, :], in_=ident[:, :], compare_op=ALU.not_equal, fill=1.0,
                               base=0, pattern=[[-1, P]], channel_multiplier=1).then_inc(s_const, 1)
            pool.wait_ge(s_const, 4)
            pool.tensor_copy(swap[:, 0:N], ident[:, N:P]).then_inc(s_const, 1)
            pool.tensor_copy(swap[:, N:P], ident[:, 0:N]).then_inc(s_const, 1)

            count = [0]

            def after(*instructions):
                for ins in instructions:
                    ins.then_inc(s_k, 1)
                count[0] += len(instructions)
                pool.wait_ge(s_k, count[0])

            def tt(out, a, b, op):
                return pool.tensor_tensor(out, a, b, op)

            k = [kw[:, i, :] for i in range(12)]
            a_re = a_in[:, 0].rearrange("p a n -> p (a n)")
            a_im = a_in[:, 1].rearrange("p a n -> p (a n)")
            c_re = c_in[:, 0].rearrange("p c a n -> p c (a n)")
            c_im = c_in[:, 1].rearrange("p c a n -> p c (a n)")

            def both(row):
                return row.unsqueeze(1).to_broadcast([P, 2, 2 * N])

            pool.wait_ge(s_a, 64)
            after(tt(k[0], a_re, a_re, ALU.mult), tt(k[1], a_im, a_im, ALU.mult))
            after(tt(k[2], k[0], k[1], ALU.add))
            pool.tensor_scalar(k[2], k[2], 0.5, 0.0, ALU.mult, ALU.add).then_inc(s_den, 1)
            pool.wait_ge(s_c, 64)
            after(tt(kc[:, 0], c_re, both(a_re), ALU.mult), tt(kc[:, 1], c_im, both(a_im), ALU.mult),
                  tt(kc[:, 2], c_re, both(a_im), ALU.mult), tt(kc[:, 3], c_im, both(a_re), ALU.mult))
            after(tt(kc[:, 4], kc[:, 0], kc[:, 1], ALU.add), tt(kc[:, 5], kc[:, 2], kc[:, 3], ALU.subtract))

            pool.wait_ge(s_turned, 1)
            pool.wait_ge(s_phase, 2)
            pool.nop(nofuse=True)
            for c in (2, 4):
                for i in range(8):
                    pool.tensor_scalar(tab[:, 8 * c + i, :], turned[:, 0:2, :].rearrange("p a h -> p (a h)"),
                                       float(8 * (c - 1) + i), phase[:, 0:1], ALU.mult, ALU.add).then_inc(s_pturns, 1)

            pool.wait_ge(s_rden, 1)
            after(tt(kc[:, 4], kc[:, 4], both(k[2]), ALU.mult),
                  tt(kc[:, 5], kc[:, 5], both(k[2]), ALU.mult))
            pool.wait_ge(s_sin, 1)
            after(tt(k[3], sinh[:, :], sinh[:, :], ALU.mult))
            after(pool.tensor_scalar(k[3], k[3], -2.0, 0.0, ALU.mult, ALU.add))
            pool.wait_ge(s_em, 2)
            after(tt(k[4], ep[:, :], k[3], ALU.mult), tt(k[5], ep[:, :], sin1[:, :], ALU.mult))
            after(tt(k[4], k[4], em[:, :], ALU.add))
            after(tt(kc[:, 0], kc[:, 4], both(k[4]), ALU.mult), tt(kc[:, 1], kc[:, 5], both(k[5]), ALU.mult),
                  tt(kc[:, 2], kc[:, 5], both(k[4]), ALU.mult), tt(kc[:, 3], kc[:, 4], both(k[5]), ALU.mult))
            part = [kc[:, i].rearrange("p c (a n) -> p (c a) n", a=2) for i in range(4)]
            after(tt(srcs[:, 6:10, 0, :], part[0], part[1], ALU.add),
                  tt(srcs[:, 10:14, 0, :], part[2], part[3], ALU.subtract))
            pool.tensor_scalar(srcs[:, 6:10, 1, :], srcs[:, 6:10, 0, :], -1.0, 0.0, ALU.mult, ALU.add).then_inc(s_ksrc, 1)
            pool.tensor_copy(srcs[:, 10:14, 1, :], srcs[:, 10:14, 0, :]).then_inc(s_ksrc, 1)

            pool.wait_ge(s_whole, 1)
            tt(tab[:, 8:16, :], tab[:, 8:16, :], whole[:, 1], ALU.subtract).then_inc(s_fpool, 1)
            pool.wait_ge(s_sine, 1)
            pool.wait_ge(s_mod, 8)
            tt(tab[:, 0:HIGH, P:2 * P], tab[:, 0:HIGH, P:2 * P], mod_hi[:, :, P:2 * P], ALU.mult).then_inc(s_ptab, 1)

            pool.wait_ge(s_frac, 4)
            pool.wait_ge(s_fpool, 1)
            pool.wait_ge(s_kturned, 2)
            for a in range(2):
                cols = slice(a * P, a * P + P)
                if a == 0:
                    pool.wait_ge(s_tab[0], 1)
                else:
                    pool.wait_ge(s_ptab, 1)
                for c in range(2):
                    k_a = turned[:, 6 + 2 * c + a, :]
                    tt(g_a[:, c, :, cols], tab[:, 0:HIGH, cols],
                       k_a.unsqueeze(1).to_broadcast([P, HIGH, P]), ALU.mult).then_inc(s_ga, 1)
                if a == 0:
                    for n, c in ((4, 1), (5, 4)):
                        pool.wait_ge(s_sine, n)
                        tt(tab[:, 8 * c:8 * c + 8, P:2 * P], tab[:, 8 * c:8 * c + 8, P:2 * P],
                           mod_lo[:, 8 * c - 8:8 * c, P:2 * P], ALU.mult).then_inc(s_ptab, 1)
            pool.wait_ge(s_dbc, 16)

            def newton(it, j):
                if j % 4 == 0 and exists(it, j + VAR_LEAD):
                    gg = (j + VAR_LEAD) // 4
                    q, n = gg % 2, it * 4 + gg
                    m, r = negm[:, q, :], nw[:, q, 6:8]
                    d = d_grp[:, q, :].unsqueeze(1).to_broadcast([P, 2, GC])

                    def wide(col):
                        return col.unsqueeze(2).to_broadcast([P, 2, GC])

                    pool.tensor_copy(d_grp[:, q, :], d_bc[:, bass.ds(n * GC, GC)]).then_inc(dg_done, 1)
                    pool.wait_ge(rec_done, n + 1)
                    pool.tensor_tensor(nw[:, q, 0:2], r0[:, q, :], r0[:, q, :], ALU.mult).then_inc(nw_done, 1)
                    pool.wait_ge(nw_done, n * 6 + 1)
                    pool.tensor_tensor(nw[:, q, 2:4], nw[:, q, 0:2], ve[:, q, :], ALU.mult).then_inc(nw_done, 1)
                    pool.wait_ge(nw_done, n * 6 + 2)
                    pool.nop(nofuse=True)
                    pool.tensor_scalar(nw[:, q, 4:6], nw[:, q, 2:4], -0.5, 1.5, ALU.mult, ALU.add).then_inc(nw_done, 1)
                    pool.wait_ge(nw_done, n * 6 + 3)
                    pool.tensor_tensor(r, nw[:, q, 4:6], r0[:, q, :], ALU.mult).then_inc(nw_done, 1)
                    pool.wait_ge(nw_done, n * 6 + 4)
                    pool.wait_ge(dg_done, n + 1)
                    pool.tensor_tensor(nw[:, q, 8:10], r, m, ALU.mult).then_inc(nw_done, 1)
                    pool.tensor_tensor(t_coef[:, gg % 4, 0, :, :], d, wide(r), ALU.mult).then_inc(nw_done, 1)
                    pool.wait_ge(nw_done, n * 6 + 6)
                    pool.tensor_tensor(t_coef[:, gg % 4, 1, :, :], t_coef[:, gg % 4, 0, :, :], wide(m), ALU.mult
                                       ).then_inc(coef_done, 1)
                    pool.wait_ge(coef_done, n * 3 + 1)
                    pool.nop(nofuse=True)
                    pool.tensor_scalar(t_coef[:, gg % 4, 0, :, :], t_coef[:, gg % 4, 0, :, :], 1.0, None, ALU.add
                                       ).then_inc(coef_done, 1)
                    pool.tensor_scalar(u_coef[:, gg % 4, :, :], nw[:, q, 6:10].rearrange("p (c u) -> p c u", c=2),
                                       U_SCALE, None, ALU.mult).then_inc(coef_done, 1)

            def split(it, j):
                if exists(it, j + SPLIT_LEAD):
                    jj = j + SPLIT_LEAD
                    n = it * BODY + jj
                    v, k, b = jj // 2 % 8, jj // 4 % 4, jj // 2 % 2
                    pool.wait_ge(xh_done, n + 1)
                    pool.wait_ge(s1_done, least(n - 3))
                    pool.tensor_tensor(xl[:, jj % 4], u_sb[:, jj % 4], xh[:, jj % 4], ALU.subtract
                                       ).then_inc(xl_done, 1)
                    pool.wait_ge(stored[v % 4], least(it * 32 + 16 * (jj // 8)))
                    pool.nop(nofuse=True)
                    for c in (2 * (jj % 2), 2 * (jj % 2) + 1):
                        ins = pool.tensor_scalar(t_sb[:, v % 4, c, :], x_tile(v)[:, c, :],
                                                 t_coef[:, k, 0, b, c:c + 1], t_coef[:, k, 1, b, c:c + 1],
                                                 ALU.mult, ALU.add)
                    ins.then_inc(t_done, 1)

            def y_factors(it, j):
                if j % 4 == 3 and exists(it, j + 1):
                    g = it * 4 + (j + 1) // 4
                    pool.tensor_copy(y_grp[:, (j + 1) // 4 % 4, :], y_bc[:, bass.ds(g * GC, GC)]
                                     ).then_inc(y_done, 1)

            def step(it, j):
                newton(it, j)
                if not (isinstance(it, int) and BODY * it + j < 0):
                    split(it, j)
                y_factors(it, j)

            newton(0, -VAR_LEAD)
            for j in (-3, -2, -1):
                split(0, j)
            pool.wait_ge(s_ybc, 16)
            run_steps(pool, step)

        @block.scalar
        def _(act):
            act.wait_ge(s_tau, 1)
            act.activation(sin1[:, :], tau[:, 0, :], ACT.Sin, scale=TWO_PI)
            act.activation(sinh[:, :], tau[:, 0, :], ACT.Sin, scale=math.pi).then_inc(s_sin, 1)

            def copy_turned(rows):
                for r, e in rows:
                    act.activation(turned[:, r:e, :], p_turn[:, r // 4, 128 * (r % 4):128 * (r % 4) + 128 * (e - r)]
                                   .rearrange("p (r h) -> p r h", h=P), ACT.Copy).then_inc(s_turned, 1)

            act.wait_ge(s_turn, 1)
            copy_turned(((0, 4), (4, 6)))
            act.wait_ge(s_turned, 2)
            x_t = turned[:, 4:6, :].rearrange("p a h -> p (a h)")
            for b in range(HIGH):
                act.activation(mod_hi[:, b, :], x_t, ACT.Exp, scale=float(LOW * b)).then_inc(s_mod, 1)
            act.wait_ge(s_phase, 2)
            for b in range(16, 24):
                act.activation(tab[:, HIGH + b, :], turned[:, 0:2, :].rearrange("p a h -> p (a h)"),
                               ACT.Identity, scale=float(b), bias=phase[:, 0:1]).then_inc(s_turns, 1)
            for b in range(LOW):
                act.activation(mod_lo[:, b, :], x_t, ACT.Exp, scale=float(b)).then_inc(s_mod, 1)
            for c in (0, 2, 3, 1, 4):
                if c == 1:
                    act.wait_ge(s_fpool, 1)
                else:
                    act.wait_ge(s_frac, max(c, 1))
                part = tab[:, 8 * c:8 * c + 8, :]
                act.activation(part, part, ACT.Sin, scale=TWO_PI).then_inc(s_sine, 1)
                if c == 3:
                    act.wait_ge(s_kturn, 1)
                    for i in range(2):
                        act.activation(turned[:, 6 + 4 * i:10 + 4 * i, :].rearrange("p r h -> p (r h)"),
                                       p_kturn[:, 512 * i:512 * i + 512], ACT.Copy).then_inc(s_kturned, 1)

            def root(it, j):
                if j % 4 == 0 and exists(it, j + VAR_LEAD):
                    gg = (j + VAR_LEAD) // 4
                    q, n = gg % 2, it * 4 + gg
                    ps = 8 * ((gg + 1) % 2)
                    act.wait_ge(stat_ps, n + 2)
                    act.activation(ve[:, q, :], st_ps[:, ps + 4:ps + 6], ACT.Identity, bias=eps_gn[:, 0:1]
                                   ).then_inc(ve_done, 1)
                    act.wait_ge(ve_done, n + 1)
                    act.activation(sd[:, q, :], ve[:, q, :], ACT.Sqrt).then_inc(sd_done, 1)

            def deviation(it, j):
                if j % 4 == 0 and exists(it, j + MEAN_LEAD):
                    gg = (j + MEAN_LEAD) // 4
                    q, n = gg % 2, it * 4 + gg
                    means = st_ps[:, 8 * q:8 * q + 4].rearrange("p (u s) -> p u s", s=2)[:, :, 0]
                    act.wait_ge(stat_ps, n + 1)
                    act.activation(negm[:, q, :], means, ACT.Copy, scale=-1.0).then_inc(negm_done, 1)
                    act.wait_ge(negm_done, n + 1)
                    for u in range(2):
                        act.activation(sq[:, q, u:u + 1], st[:, q, 2 * u:2 * u + 1], ACT.Square,
                                       bias=negm[:, q, u:u + 1]).then_inc(dev_done, 1)
                    act.wait_ge(dev_done, n * 4 + 2)
                    for u in range(2):
                        act.activation(st[:, 1 - q, 4 + u:5 + u], sq[:, q, u:u + 1], ACT.Identity,
                                       bias=st[:, q, 2 * u + 1:2 * u + 2]).then_inc(dev_done, 1)

            def split(it, j):
                if exists(it, j + SPLIT_LEAD):
                    jj = j + SPLIT_LEAD
                    m = it * BODY + jj
                    v, k, b = jj // 2 % 8, jj // 4 % 4, jj // 2 % 2
                    act.wait_ge(coef_done, it * (3 * 4) + (3 * (jj // 4) + 3))
                    act.wait_ge(xl_done, least(m - 3))
                    c = 2 * (jj % 2)
                    act.activation(u_sb[:, jj % 4],
                                   x_tile(v)[:, c:c + 2, :].rearrange("p c (s q t) -> p (c s) t q", s=2, t=2),
                                   ACT.Identity, bias=u_coef[:, k, 1, b:b + 1], scale=u_coef[:, k, 0, b:b + 1]
                                   ).then_inc(u_done, 1)
                    act.wait_ge(u_done, m + 1)
                    act.wait_ge(s1_done, least(m - 3))
                    act.activation(xh[:, jj % 4], u_sb[:, jj % 4], ACT.Copy).then_inc(xh_done, 1)

            def z_hi(it, j):
                if exists(it, j + 1):
                    m = it * BODY + j
                    z = (j + 1) % 2
                    act.wait_ge(s1_done, m + 2)
                    act.wait_ge(s2_done, least(m * 2))
                    act.activation(zh[:, z], z_ps[:, z].rearrange("p i (a r t) -> p (i a) t r", a=2, t=2)
                                   [:, :, ::-1, ::-1], ACT.Copy, scale=Z_SCALE).then_inc(zh_done, 1)

            def step(it, j):
                root(it, j)
                if not (isinstance(it, int) and BODY * it + j < 0):
                    split(it, j)
                z_hi(it, j)
                deviation(it, j)

            act.activation(sd[:, 1, 0:1], eps_gn[:, 0:1], ACT.Sqrt)
            for i in range(2):
                hs = slice(32 * i, 32 * i + 32)
                act.wait_ge(s_mode, i + 1)
                act.activation(gb[:, hs], p_mode[:, hs, :].rearrange("p h (c a) -> p h c a", c=2), ACT.Copy
                               ).then_inc(s_gb, 1)
            deviation(0, -MEAN_LEAD)
            act.wait_ge(s_rows, 2)
            for dst, src in row_parts(1):
                act.activation(dst, src, ACT.Copy).then_inc(s_g32b, 1)
            root(0, -VAR_LEAD)
            act.wait_ge(s_g32, 2)
            act.wait_ge(s_g32b, 2)
            for n, r in enumerate((1, 3)):
                if n:
                    act.wait_ge(s_l1, n)
                act.activation(gabs, g32[:, r, :], ACT.Abs, accum_out=l1[:, r:r + 1]).then_inc(s_l1, 1)
            for n, r in enumerate((0, 2)):
                act.wait_ge(s_rl1, n + 1)
                act.activation(v16[:, r, 0, :], g32[:, r, :], ACT.Copy, scale=rl1[:, r:r + 1]).then_inc(s_hi, 1)
                if n == 0:
                    split(0, -3)
            act.wait_ge(s_mean1, 1)
            deviation(0, -VAR_LEAD)
            for j in (-2, -1):
                split(0, j)

            run_steps(act, step)

        @block.tensor
        def _(pe):
            def partition_sums(it, j):
                if j % 4 == 0 and exists(it, j + VAR_LEAD) or j == -MEAN_LEAD:
                    gg = (j + MEAN_LEAD) // 4
                    q, n = gg % 2, it * 4 + gg
                    if exists(it, j + MEAN_LEAD):
                        pe.wait_ge(agg_done, n * 2 + 2)
                    if exists(it, j + VAR_LEAD):
                        pe.wait_ge(dev_done, n * 4)
                    pe.matmul(st_ps[:, 8 * q:8 * q + 6], ones[:, :], st[:, q, :], start=True, stop=True
                              ).then_inc(stat_ps, 1)

            def first_product(it, j):
                if exists(it, j + 1):
                    jj = j + 1
                    w = jj // 4 % 2
                    if isinstance(it, int) and it == 0 and jj == 0:
                        pe.wait_ge(s_wfirst, 16)
                    elif isinstance(it, int) and it == 0 and jj == 1:
                        pe.wait_ge(w_loaded[0], 16)
                    elif jj % 4 == 0:
                        pe.wait_ge(w_loaded[w], it * 32 + 16 * (jj // 8) + 16)
                    pe.wait_ge(xl_done, it * BODY + j + 2)
                    for i in range(2):
                        row = 4 * (2 * (jj % 2) + i)
                        for t in range(2):
                            n_mm = 0
                            for s in range(2):
                                for u, half in ((xh, 0), (xh, 1), (xl, 0)):
                                    ins = pe.matmul(z_ps[:, jj % 2, i, L * t:L * t + L], u[:, jj % 4, 2 * i + s, t, :],
                                                    W[:, w, row + half, s:s + L], start=n_mm == 0, stop=n_mm == 5)
                                    n_mm += 1
                    ins.then_inc(s1_done, 1)

            def second_product(it, j):
                if exists(it, j):
                    w = j // 4 % 2
                    pe.wait_ge(zl_done, it * BODY + j + 1)
                    for i in range(2):
                        row = 4 * (2 * (j % 2) + i) + 2
                        pe.wait_ge(y_free, it * (2 * BODY) + 2 * j + i + 1)
                        for s in range(2):
                            n_mm = 0
                            for t in range(2):
                                for z, half in ((zh, 0), (zh, 1), (zl, 0)):
                                    ins = pe.matmul(y_ps[:, i, L * s:L * s + L], z[:, j % 2, 2 * i + t, s, :],
                                                    W[:, w, row + half, t:t + L], start=n_mm == 0, stop=n_mm == 5)
                                    n_mm += 1
                        ins.then_inc(s2_done, 1)

            def keep_clock_up(n):
                for _ in range(n):
                    pe.matmul(warm_ps[:, :], ident[:, :], turned[:, 0:4, :].rearrange("p r h -> p (r h)"),
                              start=True, stop=True)

            pe.wait_ge(s_const, 6)
            pe.wait_ge(s_st, 1)
            pe.wait_ge(s_srcs, 4)
            for r in range(6):
                ins = pe.transpose(p_turn[:, r // 4, 128 * (r % 4):128 * (r % 4) + 128],
                                   srcs[:, r].rearrange("p a n -> p (a n)"), ident[:, :])
            ins.then_inc(s_turn, 1)
            pe.wait_ge(s_ksrc, 2)
            for r in range(8):
                ins = pe.transpose(p_kturn[:, 128 * r:128 * r + 128],
                                   srcs[:, 6 + r].rearrange("p a n -> p (a n)"), ident[:, :])
            ins.then_inc(s_kturn, 1)
            pe.wait_ge(s_turned, 2)
            for a in range(2):
                if a == 0:
                    pe.wait_ge(s_tab[0], 1)
                else:
                    pe.wait_ge(s_ptab, 1)
                for i in range(2):
                    ins = pe.matmul(p_turn[:, 2 * a + i, :].rearrange("p (b h) -> p b h", h=P), swap[:, :],
                                    tab[:, 4 * i:4 * i + 4, a * P:a * P + P], start=True, stop=True)
                ins.then_inc(s_swap, 1)
            keep_clock_up(3)
            pe.wait_ge(s_kturned, 2)
            for a in range(2):
                pe.wait_ge(s_tab[a], 5 if a == 0 else 2)
                if a == 1:
                    pe.wait_ge(s_ptab, 3)
                pe.wait_ge(s_g, a + 1)
                for n in range(C):
                    hs, e = n // 2, n % 2
                    h, q = e * (C // 2) + hs, 32 * (2 * a + e)
                    ins = pe.matmul(p_mode[q:q + 32, hs, :], tab[:, HIGH:, a * P + h],
                                    g_b[:, :, :, a * P + h], start=True, stop=True)
                    if a == 1 and n % 64 == 63:
                        ins.then_inc(s_mode, 1)
            partition_sums(0, -MEAN_LEAD)
            pe.wait_ge(s_gb, 2)
            for c in range(2):
                for a in range(HIGH):
                    ins = pe.transpose(p_rows[:, c, a, :], gb[:, :, c, a], ident[:, :])
                ins.then_inc(s_rows, 1)
            pe.wait_ge(dev_done, 4)
            pe.matmul(st_ps[:, 12:14], ones[:, :], st[:, 1, 4:6], start=True, stop=True).then_inc(stat_ps, 1)
            pe.wait_ge(agg_done, 4)
            pe.wait_ge(ve_done, 1)
            pe.matmul(st_ps[:, 8:12], ones[:, :], st[:, 1, 0:4], start=True, stop=True).then_inc(s_mean1, 1)
            pe.wait_ge(s_v16, 2)
            keep_clock_up(4)
            pe.wait_ge(s_g32b, 2)
            pe.wait_ge(s_g32, 2)

            def step(it, j):
                partition_sums(it, j)
                first_product(it, j)
                second_product(it, j)

            run_steps(pe, step)

        @block.vector
        def _(dve):
            count = [0]

            def chain(ins):
                count[0] += 1
                ins.then_inc(s_v, 1)
                dve.wait_ge(s_v, count[0])

            def exp_parts(src, res, power, w):
                k, r = w
                chain(dve.tensor_scalar(r, src, -87.0, 88.0, ALU.max, ALU.min))
                chain(dve.tensor_scalar(k, r, 1.0 / math.log(2.0), MAGIC, ALU.mult, ALU.add))
                chain(dve.tensor_scalar(k, k, MAGIC, None, ALU.subtract))
                chain(dve.scalar_tensor_tensor(r, k, -LN2_HI, r, ALU.mult, ALU.add))
                chain(dve.scalar_tensor_tensor(r, k, -LN2_LO, r, ALU.mult, ALU.add))
                chain(dve.tensor_scalar(power.bitcast(I32), k, 127.0, float(2 ** 23), ALU.add, ALU.mult))
                chain(dve.tensor_scalar(res, r, 1.0 / 5040.0, None, ALU.mult))
                for f in (720.0, 120.0, 24.0, 6.0, 2.0, 1.0):
                    chain(dve.scalar_tensor_tensor(res, res, 1.0 / f, r, ALU.add, ALU.mult))

            def sums(it, j):
                if exists(it, j + STAT_LEAD):
                    jj = j + STAT_LEAD
                    v, q, u, c = jj // 2 % 8, jj // 4 % 2, jj // 2 % 2, 2 * (jj % 2)
                    if c == 0:
                        dve.wait_ge(x_loaded[v], it * 16 + 16 * (jj // BODY) + 16)
                    for i in range(2):
                        dve.bn_stats(bst[:, q, u, c + i, :], x_tile(v)[:, c + i, :]).then_inc(bn_done, 1)
                    if c == 2:
                        dve.wait_ge(bn_done, it * (2 * BODY) + 2 * jj + 2)
                        dve.nop(nofuse=True)
                        dve.bn_aggr(st[:, q, 2 * u:2 * u + 2], bst[:, q, u].rearrange("p c s -> p (c s)")
                                    ).then_inc(agg_done, 1)

            def root_reciprocal(it, j):
                if j % 4 == 0 and exists(it, j + VAR_LEAD):
                    gg = (j + VAR_LEAD) // 4
                    dve.wait_ge(sd_done, it * 4 + gg + 1)
                    dve.reciprocal(r0[:, gg % 2, :], sd[:, gg % 2, :]).then_inc(rec_done, 1)

            w0, w1, w2 = (wk[:, i, :] for i in range(3))
            dve.memset(phase[0:N, :], 0.25).then_inc(s_phase, 1)
            dve.memset(phase[N:P, :], 0.0).then_inc(s_phase, 1)
            dve.memset(st[:, 0, 4:6], 0.0).then_inc(s_st, 1)
            dve.wait_ge(s_ldt, 32)
            exp_parts(ldt[:, :], dt[:, :], dt_pow[:, :], (wk[:, 0, 0:2], wk[:, 1, 0:2]))
            chain(dve.scalar_tensor_tensor(dt[:, :], dt[:, :], 1.0, dt_pow[:, :], ALU.add, ALU.mult))
            dve.wait_ge(s_a, 64)
            for a in range(2):
                dve.tensor_scalar(xz[:, a * N:a * N + N], a_in[:, 0, a, :], dt[:, a:a + 1], None, ALU.mult)
                dve.tensor_scalar(th[:, 0, a * N:a * N + N], a_in[:, 1, a, :], dt[:, a:a + 1], None, ALU.mult)
                chain(dve.tensor_scalar(th[:, 1, a * N:a * N + N], a_in[:, 1, a, :], dt[:, a:a + 1], float(LOW),
                                        ALU.mult, ALU.mult))
            chain(dve.tensor_scalar(turns[:, :, :], th[:, :, :], 1.0 / TWO_PI, MAGIC, ALU.mult, ALU.add))
            chain(dve.tensor_scalar(turns[:, :, :], turns[:, :, :], MAGIC, None, ALU.subtract))
            chain(dve.scalar_tensor_tensor(tau[:, :, :], turns[:, :, :], -TP1, th[:, :, :], ALU.mult, ALU.add))
            chain(dve.scalar_tensor_tensor(tau[:, :, :], turns[:, :, :], -TP2, tau[:, :, :], ALU.mult, ALU.add))
            chain(dve.scalar_tensor_tensor(tau[:, :, :], turns[:, :, :], -TP3, tau[:, :, :], ALU.mult, ALU.add))
            chain(dve.tensor_scalar(tau[:, :, :], tau[:, :, :], 1.0 / TWO_PI, -0.5, ALU.mult, ALU.max))
            dve.tensor_scalar(tau[:, :, :], tau[:, :, :], 0.5, None, ALU.min).then_inc(s_tau, 1)
            dve.wait_ge(s_tau, 1)
            for h in range(2):
                dve.tensor_copy(srcs[:, 0:4, h, :], tau[:, :, :].rearrange("p l (a n) -> p (l a) n", a=2)
                                ).then_inc(s_srcs, 1)
                dve.tensor_copy(srcs[:, 4:6, h, :], xz[:, :].rearrange("p (a n) -> p a n", a=2)
                                ).then_inc(s_srcs, 1)
            dve.wait_ge(s_den, 1)
            dve.reciprocal(kw[:, 2, :], kw[:, 2, :]).then_inc(s_rden, 1)
            exp_parts(xz[:, :], em[:, :], w2, (w0, w1))
            chain(dve.tensor_tensor(em[:, :], em[:, :], w2, ALU.mult))
            dve.tensor_tensor(ep[:, :], em[:, :], w2, ALU.add).then_inc(s_em, 1)
            dve.nop(nofuse=True)
            dve.scalar_tensor_tensor(em[:, :], w2, -1.0, em[:, :], ALU.add, ALU.add).then_inc(s_em, 1)

            dve.wait_ge(s_turned, 1)
            dve.wait_ge(s_phase, 2)
            for c in range(5):
                part = tab[:, 8 * c:8 * c + 8, :]
                if c < 2:
                    src = turned[:, (2 if c == 0 else 0):(4 if c == 0 else 2), :].rearrange("p a h -> p (a h)")
                    for b in range(8):
                        ins = dve.tensor_scalar(tab[:, 8 * c + b, :], src, float(b),
                                                phase[:, 0:1], ALU.mult, ALU.add)
                    chain(ins)
                elif c == 3:
                    dve.wait_ge(s_turns, 8)
                else:
                    dve.wait_ge(s_pturns, 4 * c)
                if c == 1:
                    dve.tensor_scalar(whole[:, 1], part, MAGIC, MAGIC, ALU.add, ALU.subtract).then_inc(s_whole, 1)
                else:
                    chain(dve.tensor_scalar(whole[:, 0], part, MAGIC, MAGIC, ALU.add, ALU.subtract))
                    dve.tensor_tensor(part, part, whole[:, 0], ALU.subtract).then_inc(s_frac, 1)
                    dve.wait_ge(s_frac, max(c, 1))
            e_x = p_turn[:, :, :].rearrange("p (a i) (b h) -> p a (i b) h", a=2, h=P)
            dve.wait_ge(s_mod, 40)

            def table(a, c, n):
                cols = slice(a * P, a * P + P)
                dve.wait_ge(s_sine, n)
                part = tab[:, 8 * c:8 * c + 8, cols]
                m = mod_hi[:, :, cols] if c == 0 else mod_lo[:, 8 * c - 8:8 * c, cols]
                dve.tensor_tensor(part, part, m, ALU.mult).then_inc(s_tab[a], 1)

            table(0, 0, 1)
            table(0, 2, 2)
            table(0, 3, 3)
            table(0, 1, 4)
            table(0, 4, 5)
            for a in range(2):
                cols = slice(a * P, a * P + P)
                if a == 0:
                    dve.wait_ge(s_tab[0], 5)
                else:
                    table(1, 2, 2)
                    table(1, 3, 3)
                    dve.wait_ge(s_tab[1], 2)
                    dve.wait_ge(s_ptab, 3)
                dve.wait_ge(s_swap, a + 1)
                dve.wait_ge(s_kturned, 2)
                for c in range(2):
                    k_b = turned[:, 10 + 2 * c + a, :]
                    ins = dve.tensor_tensor(g_b[:, c, :, cols], e_x[:, a, :, :],
                                            k_b.unsqueeze(1).to_broadcast([P, HIGH, P]), ALU.mult)
                chain(ins)
                dve.wait_ge(s_ga, 2 * a + 2)
                dve.tensor_tensor(g_b[:, :, :, cols], g_b[:, :, :, cols], g_a[:, :, :, cols], ALU.add
                                  ).then_inc(s_g, 1)
            for j in range(-12, -4):
                sums(0, j)

            dve.wait_ge(s_rows, 1)
            for dst, src in row_parts(0):
                dve.tensor_copy(dst, src).then_inc(s_g32, 1)
            dve.wait_ge(s_g32, 2)
            dve.wait_ge(s_g32b, 2)
            for e in range(2):
                r = 2 * e
                rows = slice(r, r + 2)
                dve.tensor_reduce(l1[:, r:r + 1], g32[:, r, :], AX.X, ALU.add, apply_absolute_value=True
                                  ).then_inc(s_l1v, 1)
                if e == 0:
                    root_reciprocal(0, -VAR_LEAD)
                dve.wait_ge(s_l1v, e + 1)
                dve.wait_ge(s_l1, e + 1)
                chain(dve.tensor_scalar(l1[:, rows], l1[:, rows], TINY, None, ALU.max))
                chain(dve.reciprocal(rl1[:, rows], l1[:, rows]))
                dve.tensor_scalar(rl1[:, rows], rl1[:, rows], T_SCALE, None, ALU.mult).then_inc(s_rl1, 1)
                dve.wait_ge(s_rl1, e + 1)
                chain(dve.tensor_scalar(v16[:, r + 1, 0, :], g32[:, r + 1, :], rl1[:, r + 1:r + 2], None, ALU.mult))
                for row in (r + 1, r):
                    if row == r:
                        dve.wait_ge(s_hi, e + 1)
                    dve.scalar_tensor_tensor(v16[:, row, 1, :], g32[:, row, :], rl1[:, row:row + 1],
                                             v16[:, row, 0, :], ALU.mult, ALU.subtract).then_inc(s_v16, 1)
            l1_v = l1[:, :].rearrange("p (e x) -> p x e", e=2)
            dve.scalar_tensor_tensor(yf[:, :], l1_v[:, 0, :], Y_SCALE, l1_v[:, 1, :], ALU.mult, ALU.mult
                                     ).then_inc(s_yf, 1)
            dve.engine_nop().then_inc(y_free, 2)
            for j in (-4, -3, -2):
                sums(0, j)

            def z_lo(it, j):
                if exists(it, j + 1):
                    k = (j + 1) % 2
                    dve.wait_ge(zh_done, it * BODY + j + 2)
                    z_v = z_ps[:, k].rearrange("p i (a r t) -> p (i a) t r", a=2, t=2)
                    for s in range(2):
                        ins = dve.scalar_tensor_tensor(zl[:, k, :, s, :], z_v[:, :, 1 - s, ::-1], Z_SCALE,
                                                       zh[:, k, :, s, :], ALU.mult, ALU.subtract)
                    ins.then_inc(zl_done, 1)

            def results(it, j):
                if exists(it, j):
                    v, k = j // 2 % 4, j // 4
                    dve.wait_ge(t_done, it * BODY + j + 1)
                    dve.wait_ge(y_done, it * 4 + j // 4 + 1)
                    for i in range(2):
                        c = 2 * (j % 2) + i
                        t_v = t_sb[:, v, c, :].rearrange("p (s w) -> p s w", s=2)
                        y_v = y_ps[:, i, :].rearrange("p (s w) -> p s w", s=2)[:, :, ::-1]
                        dve.wait_ge(s2_done, it * (2 * BODY) + 2 * j + i + 1)
                        dve.scalar_tensor_tensor(t_v, y_v, y_grp[:, k, c:c + 1], t_v,
                                                 ALU.mult, ALU.add).then_inc(y_free, 1)

            def step(it, j):
                sums(it, j)
                root_reciprocal(it, j)
                z_lo(it, j)
                results(it, j)

            run_steps(dve, step)

    return nc


_INS = ["x", "L0_conv_D", "L0_conv_A_re0", "L0_conv_A_re1", "L0_conv_A_im0", "L0_conv_A_im1",
        "L0_conv_C_re0", "L0_conv_C_re1", "L0_conv_C_im0", "L0_conv_C_im1",
        "L0_conv_log_dt0", "L0_conv_log_dt1"]


def kernel(**inputs):
    import numpy as np
    import concourse.bacc as bacc
    from concourse.bass_utils import run_bass_kernel_spmd

    nc = bacc.Bacc("TRN2", target_bir_lowering=False, num_devices=1)
    arrays, args = {}, []
    for name in _INS:
        a = np.ascontiguousarray(inputs[name])
        arrays[f"in_{name}"] = a
        args.append(nc.dram_tensor(f"in_{name}", a.shape, mybir.dt.from_np(a.dtype), kind="ExternalInput").ap())
    out = nc.dram_tensor("out", (B, C, L, L), F32, kind="ExternalOutput").ap()
    x, d, ar0, ar1, ai0, ai1, cr0, cr1, ci0, ci1, l0, l1 = args
    conv_block(nc, x, d.rearrange("o h -> (o h)"), (ar0, ar1), (ai0, ai1), (cr0, cr1), (ci0, ci1), (l0, l1), out)
    result = run_bass_kernel_spmd(nc, [arrays], core_ids=[0])
    return result.results[0]["out"]
```
